# Optimizing a Trainium2 kernel written in Bass

```python
import numpy as np
import jax
import jax.numpy as jnp

def _softmax(x, axis=-1):
    return jax.nn.softmax(x, axis=axis)

def _gelu(x):
    return jax.nn.gelu(x, approximate=True)

def _silu(x):
    return jax.nn.silu(x)

def _sigmoid(x):
    return jax.nn.sigmoid(x)

def _layernorm(x, axis=-1, eps=1e-05):
    m = jnp.mean(x, axis=axis, keepdims=True)
    v = jnp.var(x, axis=axis, keepdims=True)
    return (x - m) / jnp.sqrt(v + eps)

def _scatter_add(tgt, idx, src, axis=0):
    return tgt.at[idx].add(src)

def _segment_sum(src, seg, n):
    return jax.ops.segment_sum(src, seg, n)
kernel_name = 'mk_gnn_preln_d2_gnn_r32_db28fd'

def setup_inputs(seed: int=0):
    np.random.seed(seed)
    _w = jnp.asarray

    def _rec_inputs():
        import jax
        import jax.numpy as jnp
        _gk = jax.random.key(seed)
        x = -0.0003542 + 1 * jax.random.normal(jax.random.fold_in(_gk, 1), (500, 256), jnp.float32)
        _s = jax.random.randint(jax.random.fold_in(_gk, 2), (8000,), 0, 500, jnp.int32)
        _d = jax.random.randint(jax.random.fold_in(_gk, 3), (8000,), 0, 500, jnp.int32)
        _loop = jnp.arange(500, dtype=jnp.int32)
        src = jnp.concatenate([_s, _d, _loop])
        dst = jnp.concatenate([_d, _s, _loop])
        _o = jnp.argsort(dst, stable=True)
        src = src[_o]
        dst = dst[_o]
        edge_attr_128 = 4.82035e-05 + 0.999966 * jax.random.normal(jax.random.fold_in(_gk, 11), (16500, 128), jnp.float32)
        edge_attr_64 = -9.77346e-05 + 0.999888 * jax.random.normal(jax.random.fold_in(_gk, 12), (16500, 64), jnp.float32)
        edge_weight = jax.random.uniform(jax.random.fold_in(_gk, 15), (16500,), jnp.float32, 0.0, 0.999951)
        return (x, src, dst, edge_attr_128, edge_attr_64, edge_weight)
    x, src, dst, edge_attr_128, edge_attr_64, edge_weight = _rec_inputs()

    def _L0_gnn_setup():
        import jax, jax.numpy as jnp
        import numpy as np
        BN_EPS = 1e-05

        def _bn(x, gamma, beta, mean, var):
            return (x - mean) / jnp.sqrt(var + BN_EPS) * gamma + beta
        key = jax.random.key(seed)
        ks = jax.random.split(key, 24)
        N, E = (500, 2000)
        D_IN, H, D_OUT, D_E, KH = (256, 64, 256, 128, 32)
        s = 0.05
        inp = {}
        inp['x'] = jax.random.normal(ks[0], (N, D_IN), jnp.float32)
        inp['edge_input'] = jax.random.normal(ks[1], (E, D_E), jnp.float32)
        inp['edge_list'] = jax.random.randint(ks[2], (E, 2), 0, N, jnp.int32)
        inp['edge_weight'] = jax.random.uniform(ks[3], (E,), jnp.float32)
        inp['w1'] = jax.random.normal(ks[4], (D_IN, H), jnp.float32) * s
        inp['b1'] = jax.random.normal(ks[5], (H,), jnp.float32) * s
        inp['kw1'] = jax.random.normal(ks[6], (D_E, KH), jnp.float32) * s
        inp['kb1'] = jax.random.normal(ks[7], (KH,), jnp.float32) * s
        inp['kw2'] = jax.random.normal(ks[8], (KH, (H + 1) * H), jnp.float32) * s
        inp['kb2'] = jax.random.normal(ks[9], ((H + 1) * H,), jnp.float32) * s
        inp['w2'] = jax.random.normal(ks[10], (H, D_OUT), jnp.float32) * s
        inp['b2'] = jax.random.normal(ks[11], (D_OUT,), jnp.float32) * s

        def bn_params(k, d):
            k1, k2, k3, k4 = jax.random.split(k, 4)
            g = 1.0 + jax.random.normal(k1, (d,), jnp.float32) * s
            b = jax.random.normal(k2, (d,), jnp.float32) * s
            m = jax.random.normal(k3, (d,), jnp.float32) * s
            v = 0.5 + jax.random.uniform(k4, (d,), jnp.float32)
            return (g, b, m, v)
        inp['g_in'], inp['be_in'], inp['m_in'], inp['v_in'] = bn_params(ks[12], D_IN)
        inp['g_msg'], inp['be_msg'], inp['m_msg'], inp['v_msg'] = bn_params(ks[13], H)
        inp['g_upd'], inp['be_upd'], inp['m_upd'], inp['v_upd'] = bn_params(ks[14], H)
        inp['g_out'], inp['be_out'], inp['m_out'], inp['v_out'] = bn_params(ks[15], D_OUT)
        return inp
    _L0_gnn_all = _L0_gnn_setup()
    _L0_gnn_in = {k: v for k, v in _L0_gnn_all.items() if k in ('w1', 'b1', 'kw1', 'kb1', 'kw2', 'kb2', 'w2', 'b2', 'g_in', 'be_in', 'm_in', 'v_in', 'g_msg', 'be_msg', 'm_msg', 'v_msg', 'g_upd', 'be_upd', 'm_upd', 'v_upd', 'g_out', 'be_out', 'm_out', 'v_out')}
    del _L0_gnn_all

    def _L1_gnn_setup():
        import jax, jax.numpy as jnp
        import numpy as np
        import math
        N, E = (50000, 25000)
        IN_CH, EDGE_DIM, H, C = (256, 64, 8, 32)
        key = jax.random.key(seed)
        ks = jax.random.split(key, 12)

        def xavier(k, shape):
            fan_in, fan_out = (shape[0], shape[1])
            a = math.sqrt(6.0 / (fan_in + fan_out))
            return jax.random.uniform(k, shape, jnp.float32, -a, a)
        x = jax.random.normal(ks[0], (N, IN_CH), jnp.float32)
        edge_attr = jax.random.normal(ks[1], (E, EDGE_DIM), jnp.float32)
        edge_index = jax.random.randint(ks[2], (2, E), 0, N, jnp.int64)
        Wq = xavier(ks[3], (IN_CH, H * C))
        bq = jnp.zeros((H * C,), jnp.float32)
        Wk = xavier(ks[4], (IN_CH, H * C))
        bk = jnp.zeros((H * C,), jnp.float32)
        Wv = xavier(ks[5], (IN_CH, H * C))
        bv = jnp.zeros((H * C,), jnp.float32)
        We = xavier(ks[6], (EDGE_DIM, H * C))
        be = jnp.zeros((H * C,), jnp.float32)
        bias = jnp.zeros((H * C,), jnp.float32)
        return {'x': x, 'edge_attr': edge_attr, 'Wq': Wq, 'bq': bq, 'Wk': Wk, 'bk': bk, 'Wv': Wv, 'bv': bv, 'We': We, 'be': be, 'bias': bias, 'edge_index': edge_index}
    _L1_gnn_all = _L1_gnn_setup()
    _L1_gnn_in = {k: v for k, v in _L1_gnn_all.items() if k in ('Wq', 'bq', 'Wk', 'bk', 'Wv', 'bv', 'We', 'be', 'bias')}
    del _L1_gnn_all
    return {'x': x, 'src': src, 'dst': dst, 'edge_attr_128': edge_attr_128, 'edge_attr_64': edge_attr_64, 'edge_weight': edge_weight, 'L0_gnn_w1': _L0_gnn_in['w1'], 'L0_gnn_b1': _L0_gnn_in['b1'], 'L0_gnn_kw1': _L0_gnn_in['kw1'], 'L0_gnn_kb1': _L0_gnn_in['kb1'], 'L0_gnn_kw2': _L0_gnn_in['kw2'], 'L0_gnn_kb2': _L0_gnn_in['kb2'], 'L0_gnn_w2': _L0_gnn_in['w2'], 'L0_gnn_b2': _L0_gnn_in['b2'], 'L0_gnn_g_in': _L0_gnn_in['g_in'], 'L0_gnn_be_in': _L0_gnn_in['be_in'], 'L0_gnn_m_in': _L0_gnn_in['m_in'], 'L0_gnn_v_in': _L0_gnn_in['v_in'], 'L0_gnn_g_msg': _L0_gnn_in['g_msg'], 'L0_gnn_be_msg': _L0_gnn_in['be_msg'], 'L0_gnn_m_msg': _L0_gnn_in['m_msg'], 'L0_gnn_v_msg': _L0_gnn_in['v_msg'], 'L0_gnn_g_upd': _L0_gnn_in['g_upd'], 'L0_gnn_be_upd': _L0_gnn_in['be_upd'], 'L0_gnn_m_upd': _L0_gnn_in['m_upd'], 'L0_gnn_v_upd': _L0_gnn_in['v_upd'], 'L0_gnn_g_out': _L0_gnn_in['g_out'], 'L0_gnn_be_out': _L0_gnn_in['be_out'], 'L0_gnn_m_out': _L0_gnn_in['m_out'], 'L0_gnn_v_out': _L0_gnn_in['v_out'], 'L1_gnn_Wq': _L1_gnn_in['Wq'], 'L1_gnn_bq': _L1_gnn_in['bq'], 'L1_gnn_Wk': _L1_gnn_in['Wk'], 'L1_gnn_bk': _L1_gnn_in['bk'], 'L1_gnn_Wv': _L1_gnn_in['Wv'], 'L1_gnn_bv': _L1_gnn_in['bv'], 'L1_gnn_We': _L1_gnn_in['We'], 'L1_gnn_be': _L1_gnn_in['be'], 'L1_gnn_bias': _L1_gnn_in['bias']}

def reference(x, src, dst, edge_attr_128, edge_attr_64, edge_weight, L0_gnn_w1, L0_gnn_b1, L0_gnn_kw1, L0_gnn_kb1, L0_gnn_kw2, L0_gnn_kb2, L0_gnn_w2, L0_gnn_b2, L0_gnn_g_in, L0_gnn_be_in, L0_gnn_m_in, L0_gnn_v_in, L0_gnn_g_msg, L0_gnn_be_msg, L0_gnn_m_msg, L0_gnn_v_msg, L0_gnn_g_upd, L0_gnn_be_upd, L0_gnn_m_upd, L0_gnn_v_upd, L0_gnn_g_out, L0_gnn_be_out, L0_gnn_m_out, L0_gnn_v_out, L1_gnn_Wq, L1_gnn_bq, L1_gnn_Wk, L1_gnn_bk, L1_gnn_Wv, L1_gnn_bv, L1_gnn_We, L1_gnn_be, L1_gnn_bias):
    import jax
    import jax.numpy as jnp

    def _L0_gnn_ref(x, edge_input, edge_list, edge_weight, w1, b1, kw1, kb1, kw2, kb2, w2, b2, g_in, be_in, m_in, v_in, g_msg, be_msg, m_msg, v_msg, g_upd, be_upd, m_upd, v_upd, g_out, be_out, m_out, v_out):
        import jax, jax.numpy as jnp
        import numpy as np
        BN_EPS = 1e-05

        def _bn(x, gamma, beta, mean, var):
            return (x - mean) / jnp.sqrt(var + BN_EPS) * gamma + beta
        N = x.shape[0]
        H = w1.shape[1]
        node_in = edge_list[:, 0]
        node_out = edge_list[:, 1]
        xn = _bn(x, g_in, be_in, m_in, v_in)
        layer_input = jax.nn.relu(xn)
        msg = layer_input[node_in] @ w1 + b1
        msg = jax.nn.relu(_bn(msg, g_msg, be_msg, m_msg, v_msg))
        kern = jax.nn.relu(edge_input @ kw1 + kb1) @ kw2 + kb2
        kern = kern.reshape(-1, H + 1, H)
        msg = jnp.einsum('ejk,ek->ej', kern[:, 1:, :], msg) + kern[:, 0, :]
        update = jax.ops.segment_sum(msg * edge_weight[:, None], node_out, num_segments=N)
        update = jax.nn.relu(_bn(update, g_upd, be_upd, m_upd, v_upd))
        out = update @ w2 + b2
        out = _bn(out, g_out, be_out, m_out, v_out)
        return out

    def _L1_gnn_ref(x, edge_attr, Wq, bq, Wk, bk, Wv, bv, We, be, bias, edge_index):
        import jax, jax.numpy as jnp
        import numpy as np
        import math
        N, E = (50000, 25000)
        IN_CH, EDGE_DIM, H, C = (256, 64, 8, 32)
        n = x.shape[0]
        q = (x @ Wq + bq).reshape(n, H, C)
        k = (x @ Wk + bk).reshape(n, H, C)
        v = (x @ Wv + bv).reshape(n, H, C)
        dst = edge_index[0]
        src = edge_index[1]
        e = (edge_attr @ We + be).reshape(-1, H, C)
        key_j = k[src] + e
        alpha = (q[dst] * key_j).sum(-1) / math.sqrt(C)
        alpha = jax.nn.softmax(alpha, axis=0)
        out = v[src] * alpha[:, :, None]
        out = jax.ops.segment_sum(out, dst, num_segments=n)
        return out.reshape(n, H * C) + bias
    edge_index = jnp.stack([src, dst])
    edge_index_t = jnp.stack([src, dst], axis=1)
    h = jnp.maximum(_layernorm(x, axis=-1), 0.0)
    x = x + _L0_gnn_ref(h, edge_attr_128, edge_index_t, edge_weight, L0_gnn_w1, L0_gnn_b1, L0_gnn_kw1, L0_gnn_kb1, L0_gnn_kw2, L0_gnn_kb2, L0_gnn_w2, L0_gnn_b2, L0_gnn_g_in, L0_gnn_be_in, L0_gnn_m_in, L0_gnn_v_in, L0_gnn_g_msg, L0_gnn_be_msg, L0_gnn_m_msg, L0_gnn_v_msg, L0_gnn_g_upd, L0_gnn_be_upd, L0_gnn_m_upd, L0_gnn_v_upd, L0_gnn_g_out, L0_gnn_be_out, L0_gnn_m_out, L0_gnn_v_out)
    h = jnp.maximum(_layernorm(x, axis=-1), 0.0)
    x = x + _L1_gnn_ref(h, edge_attr_64, L1_gnn_Wq, L1_gnn_bq, L1_gnn_Wk, L1_gnn_bk, L1_gnn_Wv, L1_gnn_bv, L1_gnn_We, L1_gnn_be, L1_gnn_bias, edge_index)
    return x

_drawn_inputs = setup_inputs


def setup_inputs(seed=0):
    import zlib

    import numpy as np

    out = dict(_drawn_inputs(seed))
    spreads = {'L1_gnn_bq': (0.0, 0.8),
     'L1_gnn_bk': (0.0, 2.0),
     'L1_gnn_bv': (0.0, 2.0),
     'L1_gnn_be': (0.0, 2.0),
     'L1_gnn_bias': (0.0, 0.1)}
    factors = {'edge_attr_64': 8.0,
     'L0_gnn_be_upd': 5.49,
     'L0_gnn_m_upd': 5.231,
     'L1_gnn_Wq': 8.0,
     'L1_gnn_Wk': 8.0,
     'L1_gnn_Wv': 8.0,
     'L1_gnn_We': 8.0}
    for name, (base, spread) in spreads.items():
        noise = np.random.default_rng([zlib.crc32(name.encode()), seed]).standard_normal(out[name].shape)
        drawn = base * np.exp(spread * noise) if base else spread * noise
        out[name] = jnp.asarray(drawn.astype(out[name].dtype))
    for name, factor in factors.items():
        out[name] = (out[name] * factor).astype(out[name].dtype)
    return out
```

```python
import concourse.bass as bass
from concourse import mybir
from contextlib import ExitStack


N, E = 500, 16500
D, DE0, DE1 = 256, 128, 64
H0, KH = 64, 32
HEADS, C = 8, 32
EPS = 1e-5
P = 128
NB, NP = 4, 125
A = 3
PAIRS = -(-E // (P * A * 2))
GR = 2 * PAIRS
CH = GR * A
EP = CH * P
WIN = 8
KI = KH + 1
XW = KI * WIN
CS = CH * WIN
ROUNDS = -(-N // WIN)
THIRD = CS // 3
PC = 96
NPC = CS // PC
VECS0 = ["g_in", "be_in", "m_in", "v_in", "g_out", "be_out", "m_out", "v_out", "b2"]
VECS1 = ["bq", "bk", "bv", "be", "bias"]
assert N == NB * NP and THIRD <= 512 and CS % PC == 0 and CS % 3 == 0

F = mybir.dt.float32
FR = mybir.dt.float32r
I32 = mybir.dt.int32
ALU = mybir.AluOpType
ACT = mybir.ActivationFunctionType
AX = mybir.AxisListType.X


class Chain:

    def __init__(self, eng, sem):
        self.eng, self.sem, self.n = eng, sem, 0

    def __call__(self, ins):
        self.n += 1
        ins.then_inc(self.sem, 1)
        return ins

    def wait(self):
        self.eng.wait_ge(self.sem, self.n)

    def link(self, ins):
        self(ins)
        self.wait()


def ds(start, size):
    return bass.ds(start, size)


def normalised(nc, eng, ch, sqrt_in, sqrt_done, tiles, xin, hout, n, ready=None):
    mean, var, rs, tmp, sq = tiles
    ch.link(nc.vector.tensor_reduce(mean[:, :], xin[:, :, :], AX, ALU.add))
    ch.link(nc.vector.tensor_scalar(mean[:, :], mean[:, :], 1.0 / D, None, ALU.mult))
    ch.link(nc.vector.tensor_tensor(hout[:, :, :], xin[:, :, :], mean[:, :].unsqueeze(2).to_broadcast([NP, NB, D]), ALU.subtract))
    ch.link(nc.vector.tensor_tensor(sq[:, :, :], hout[:, :, :], hout[:, :, :], ALU.mult))
    ch.link(nc.vector.tensor_reduce(var[:, :], sq[:, :, :], AX, ALU.add))
    nc.vector.tensor_scalar(var[:, :], var[:, :], 1.0 / D, EPS, ALU.mult, ALU.add).then_inc(sqrt_in, 1)
    eng.wait_ge(sqrt_done, n)
    rsqrt_refined(nc, ch, rs[:, :], var[:, :], tmp[:, :])
    ch.link(nc.vector.tensor_tensor(hout[:, :, :], hout[:, :, :], rs[:, :].unsqueeze(2).to_broadcast([NP, NB, D]), ALU.mult))
    last = nc.vector.tensor_scalar(hout[:, :, :], hout[:, :, :], 0.0, None, ALU.max)
    if ready is None:
        ch.link(last)
    else:
        last.then_inc(ready, 1)


def rsqrt_refined(nc, ch, rs, v, tmp):
    ch.wait()
    ch.link(nc.vector.reciprocal(rs, rs))
    ch.link(nc.vector.tensor_tensor(tmp, rs, rs, ALU.mult))
    ch.link(nc.vector.tensor_tensor(tmp, tmp, v, ALU.mult))
    ch.link(nc.vector.tensor_scalar(tmp, tmp, -0.5, 1.5, ALU.mult, ALU.add))
    ch.link(nc.vector.tensor_tensor(rs, rs, tmp, ALU.mult))


def build(nc, a, out):
    mtab = nc.dram_tensor("mtab", [N, 2 * H0], F, kind="Internal").ap()
    ktab = nc.dram_tensor("ktab", [N, D], F, kind="Internal").ap()
    vtab = nc.dram_tensor("vtab", [N, D], F, kind="Internal").ap()
    lo_d = nc.dram_tensor("lo_d", [CH], F, kind="Internal").ap()
    span_d = nc.dram_tensor("span_d", [CH], I32, kind="Internal").ap()
    node_d = nc.dram_tensor("node_d", [CS], F, kind="Internal").ap()
    ctx = ExitStack()
    with ctx:
        def sb(name, shape, dt=F, c=ctx):
            return c.enter_context(nc.sbuf_tensor(name, shape, dt))

        class Shared:
            pass

        s = Shared()
        psum = ctx.enter_context(nc.psum_tensor("psum", [P, 8, 512], F))
        s.ps = [psum[:, i, :] for i in range(8)]
        s.banks3 = lambda u: psum[:, A * u:A * u + A, :]
        s.ident = sb("ident", [P, P])
        s.xres = sb("xres", [NP, NB, D])
        s.src_i = sb("src_i", [P, CH], I32)
        s.dst_i = sb("dst_i", [P, CH], I32)
        s.src_f = sb("src_f", [P, CH])
        s.w = sb("w", [P, CH])
        s.dl = sb("dl", [P, CH])
        s.rounds = sb("rounds", [1, 1], I32)
        s.node = sb("node", [PC, NPC])
        s.iota_n = sb("iota_n", [P, N])
        s.iota_w = sb("iota_w", [P, WIN])
        s.updT = sb("updT", [H0, N])
        s.w2s = sb("w2s", [H0, D])
        s.upd_ab = sb("upd_ab", [H0, 2])
        s.kb1 = sb("kb1", [P, KH])
        s.kw1 = sb("kw1", [P, KH])
        s.T = sb("T", [P, KI, H0])
        s.T0 = sb("T0", [KI, H0])
        stage_nodes0(nc, a, s, mtab, lo_d, span_d, node_d)
        stage_edges0(nc, a, s, mtab)
        with ExitStack() as c:
            s.QT = sb("QT", [NP, NB, 2, D], FR, c)
            stage_nodes1(nc, a, s, ktab, vtab)
            s.alpha = sb("alpha", [P, CH, HEADS], F, c)
            s.nodeid = sb("nodeid", [NP, NB], F, c)
            stage_scores(nc, a, s, ktab)
            s.rsum = sb("rsum", [P, HEADS], F, c)
            stage_softmax(nc, a, s)
            stage_values(nc, a, s, vtab, out)


def stage_nodes0(nc, a, s, mtab, lo_d, span_d, node_d):
    with ExitStack() as ctx:
        def sb(name, shape, dt=F):
            return ctx.enter_context(nc.sbuf_tensor(name, shape, dt))

        def sem(name):
            return ctx.enter_context(nc.semaphore(name))

        s.mean = sb("mean0", [NP, NB])
        s.var = sb("var0", [NP, NB])
        s.rs = sb("rs0", [NP, NB])
        s.tmp4 = sb("tmp40", [NP, NB])
        s.h = sb("h0", [NP, NB, D])
        s.sq = sb("sq0", [NP, NB, D])
        s.hT = sb("hT0", [P, 2, NB, NP])
        vec = sb("vec0", [NP, len(VECS0), D])
        small = sb("small", [NP, 5, H0])
        vr = sb("vr", [NP, 2 * D + H0])
        vv = sb("vv", [NP, 2 * D + H0])
        vt = sb("vt", [NP, 2 * D + H0])
        cin = sb("cin", [NP, D])
        cmsg = sb("cmsg", [NP, H0])
        w1 = sb("w1", [P, 2, H0])
        ones1 = sb("ones1", [1, P])
        up = sb("up", [H0, 4])
        upt = sb("upt", [H0, 4])
        Mf = sb("Mf", [NP, NB, H0])
        Mt = sb("Mt", [NP, NB, 2 * H0], FR)
        dr = sb("dr", [GR, A, P], I32)
        drf = sb("drf", [GR, A, P])
        lo = sb("lo", [GR, A])
        hi = sb("hi", [GR, A])
        span = sb("span", [GR, A], I32)
        nodes = sb("nodes", [GR, A, WIN])
        lob = sb("lob", [P, CH])
        spans = sb("spans", [1, CH], I32)
        span1 = sb("span1", [1, 1], I32)
        x_in = sem("x_in")
        vec_in = sem("vec_in")
        dst_in = sem("dst_in")
        weights_in = sem("weights_in")
        edge_in = sem("edge_in")
        win_out = sem("win_out")
        win_in = sem("win_in")
        win_ready = sem("win_ready")
        m_out = sem("m_out")
        m_ready = sem("m_ready")
        dve = sem("dve_done")
        pool = sem("pool_done")
        sqrt_in = sem("sqrt_in")
        sqrt_done = sem("sqrt_done")
        h_ready = sem("h_ready")
        hT_done = sem("hT_done")
        hT_ready = sem("hT_ready")
        mm_done = sem("mm_done")
        block = ctx.enter_context(nc.Block())

        @block.sync
        def _(sp):
            sp.dma_start(s.h[:, :, :], a["x"].rearrange("(b p) d -> p b d", p=NP)).then_inc(x_in, 16)
            sp.dma_start(vec[:, :, :].rearrange("p a d -> p (a d)"), a["vecs0"].to_broadcast([NP, len(VECS0) * D])).then_inc(vec_in, 16)
            sp.dma_start(small[:, :, :].rearrange("p a d -> p (a d)"), a["msg_vecs"].to_broadcast([NP, 5 * H0])).then_inc(vec_in, 16)
            sp.dma_start(up[:, :], a["upd_vecs"]).then_inc(vec_in, 16)
            sp.dma_start(w1[:, :, :], a["w1"].rearrange("(k p) j -> p k j", p=P)).then_inc(weights_in, 16)
            sp.dma_start(s.w2s[:, :], a["w2"]).then_inc(weights_in, 16)
            sp.dma_start(s.w[:, :], a["w_pc"]).then_inc(edge_in, 16)
            sp.wait_ge(m_ready, 1)
            sp.dma_start(mtab.rearrange("(b p) d -> p b d", p=NP), Mt[:, :, :].bitcast(F)).then_inc(m_out, 16)
            sp.wait_ge(m_out, 16)

        @block.scalar
        def _(act):
            act.dma_start(dr[:, :, :], a["dst_rows"]).then_inc(dst_in, 16)
            act.dma_start(s.src_i[:, :], a["src_pc"]).then_inc(edge_in, 16)
            act.dma_start(s.dst_i[:, :], a["dst_pc"]).then_inc(edge_in, 16)
            act.dma_start(s.kw1[:, :], a["kw1"]).then_inc(edge_in, 16)
            act.dma_start(s.kb1[:, :], a["kb1"].to_broadcast([P, KH])).then_inc(edge_in, 16)
            act.dma_start(s.T[0:H0, :, :], a["T"]).then_inc(edge_in, 16)
            act.dma_start(s.T[H0:P, :, :], a["T"]).then_inc(edge_in, 16)
            act.dma_start(s.T0[:, :], a["T0"]).then_inc(edge_in, 16)
            act.wait_ge(win_ready, 1)
            act.dma_start(lo_d.rearrange("(g a) -> g a", a=A), lo[:, :]).then_inc(win_out, 16)
            act.dma_start(span_d.rearrange("(g a) -> g a", a=A), span[:, :]).then_inc(win_out, 16)
            act.dma_start(node_d.rearrange("(g a) -> g a", a=A * WIN), nodes[:, :, :].rearrange("g a w -> g (a w)")).then_inc(win_out, 16)
            act.wait_ge(win_out, 48)
            act.dma_start(lob[:, :], lo_d.rearrange("(o c) -> o c", o=1).to_broadcast([P, CH])).then_inc(win_in, 16)
            act.dma_start(spans[:, :], span_d.rearrange("(o c) -> o c", o=1)).then_inc(win_in, 16)
            act.dma_start(s.node[:, :], node_d.rearrange("(q j) -> q j", j=NPC)).then_inc(win_in, 16)
            act.wait_ge(sqrt_in, 1)
            act.activation(vr[:, :], vv[:, :], ACT.Sqrt).then_inc(sqrt_done, 1)
            act.activation(upt[:, 0:1], upt[:, 1:2], ACT.Sqrt).then_inc(sqrt_done, 1)
            act.wait_ge(sqrt_in, 2)
            act.activation(s.rs[:, :], s.var[:, :], ACT.Sqrt).then_inc(sqrt_done, 1)
            act.wait_ge(hT_done, 2)
            for k in range(2):
                act.activation(s.hT[:, k, :, :].rearrange("p b n -> p (b n)"), s.ps[k][:, 0:N], ACT.Copy).then_inc(hT_ready, 1)

        @block.gpsimd
        def _(pl):
            ch = Chain(pl, pool)
            ch(nc.gpsimd.memset(s.ident[:, :], 0.0))
            ch(nc.gpsimd.iota(s.iota_n[:, :], pattern=[[1, N]], base=0, channel_multiplier=0, allow_small_or_imprecise_dtypes=True))
            ch(nc.gpsimd.iota(s.iota_w[:, :], pattern=[[1, WIN]], base=0, channel_multiplier=0, allow_small_or_imprecise_dtypes=True))
            ch.wait()
            ch(nc.gpsimd.affine_select(out=s.ident[:, :], in_=s.ident[:, :], compare_op=ALU.not_equal, fill=1.0,
                                       base=0, pattern=[[-1, P]], channel_multiplier=1))

        @block.vector
        def _(ve):
            ch = Chain(ve, dve)
            nv = {n: vec[:, i, :] for i, n in enumerate(VECS0)}
            ve.wait_ge(dst_in, 16)
            ve.wait_ge(pool, 3)
            ch.link(nc.vector.tensor_copy(drf[:, :, :], dr[:, :, :]))
            ch.link(nc.vector.tensor_reduce(lo[:, :], drf[:, :, :], AX, ALU.min))
            ch.link(nc.vector.tensor_reduce(hi[:, :], drf[:, :, :], AX, ALU.max))
            ch.link(nc.vector.tensor_tensor(span[:, :], hi[:, :], lo[:, :], ALU.subtract))
            nc.vector.tensor_tensor(nodes[:, :, :], lo[:, :].unsqueeze(2).to_broadcast([GR, A, WIN]),
                                       s.iota_w[0:GR, :].unsqueeze(1).to_broadcast([GR, A, WIN]), ALU.add).then_inc(win_ready, 1)
            ve.wait_ge(vec_in, 48)
            ch(nc.vector.tensor_scalar(vv[:, 0:D], nv["v_in"], EPS, None, ALU.add))
            ch(nc.vector.tensor_scalar(vv[:, D:2 * D], nv["v_out"], EPS, None, ALU.add))
            ch(nc.vector.tensor_scalar(vv[:, 2 * D:], small[:, 3, :], EPS, None, ALU.add))
            nc.vector.tensor_scalar(upt[:, 1:2], up[:, 3:4], EPS, None, ALU.add).then_inc(sqrt_in, 1)
            ve.wait_ge(x_in, 16)
            ch.link(nc.vector.tensor_copy(s.xres[:, :, :], s.h[:, :, :]))
            normalised(nc, ve, ch, sqrt_in, sqrt_done, (s.mean, s.var, s.rs, s.tmp4, s.sq), s.xres, s.h, 3)
            rsqrt_refined(nc, ch, vr[:, :], vv[:, :], vt[:, :])
            rsqrt_refined(nc, ch, upt[:, 0:1], upt[:, 1:2], upt[:, 2:3])
            ch.link(nc.vector.tensor_tensor(vr[:, 0:D], vr[:, 0:D], nv["g_in"], ALU.mult))
            ch.link(nc.vector.tensor_tensor(cin[:, :], nv["m_in"], vr[:, 0:D], ALU.mult))
            ch.link(nc.vector.tensor_tensor(cin[:, :], nv["be_in"], cin[:, :], ALU.subtract))
            ch.link(nc.vector.tensor_tensor(s.h[:, :, :], s.h[:, :, :], vr[:, 0:D].unsqueeze(1).to_broadcast([NP, NB, D]), ALU.mult))
            ch.link(nc.vector.tensor_tensor(s.h[:, :, :], s.h[:, :, :], cin[:, :].unsqueeze(1).to_broadcast([NP, NB, D]), ALU.add))
            nc.vector.tensor_scalar(s.h[:, :, :], s.h[:, :, :], 0.0, None, ALU.max).then_inc(h_ready, 1)
            ch.link(nc.vector.tensor_tensor(vr[:, 2 * D:], vr[:, 2 * D:], small[:, 0, :], ALU.mult))
            ch.link(nc.vector.tensor_tensor(cmsg[:, :], small[:, 4, :], small[:, 2, :], ALU.subtract))
            ch.link(nc.vector.tensor_tensor(cmsg[:, :], cmsg[:, :], vr[:, 2 * D:], ALU.mult))
            ch.link(nc.vector.tensor_tensor(cmsg[:, :], cmsg[:, :], small[:, 1, :], ALU.add))
            ve.wait_ge(weights_in, 32)
            ch.link(nc.vector.tensor_tensor(vr[:, D:2 * D], vr[:, D:2 * D], nv["g_out"], ALU.mult))
            ch(nc.vector.tensor_tensor(s.w2s[:, :], s.w2s[:, :], vr[0:H0, D:2 * D], ALU.mult))
            ch.link(nc.vector.tensor_tensor(cin[:, :], nv["b2"], nv["m_out"], ALU.subtract))
            ch.link(nc.vector.tensor_tensor(cin[:, :], cin[:, :], vr[:, D:2 * D], ALU.mult))
            ch.link(nc.vector.tensor_tensor(cin[:, :], cin[:, :], nv["be_out"], ALU.add))
            ch(nc.vector.tensor_tensor(s.xres[:, :, :], s.xres[:, :, :], cin[:, :].unsqueeze(1).to_broadcast([NP, NB, D]), ALU.add))
            ch.link(nc.vector.tensor_tensor(s.upd_ab[:, 0:1], upt[:, 0:1], up[:, 0:1], ALU.mult))
            ch.link(nc.vector.tensor_tensor(upt[:, 3:4], up[:, 2:3], s.upd_ab[:, 0:1], ALU.mult))
            ch(nc.vector.tensor_tensor(s.upd_ab[:, 1:2], up[:, 1:2], upt[:, 3:4], ALU.subtract))
            ve.wait_ge(edge_in, 16 * 8)
            ch(nc.vector.tensor_copy(s.src_f[:, :], s.src_i[:, :]))
            ch.link(nc.vector.tensor_copy(s.dl[:, :], s.dst_i[:, :]))
            ve.wait_ge(win_in, 48)
            ch(nc.vector.tensor_tensor(s.dl[:, :], s.dl[:, :], lob[:, :], ALU.subtract))
            ch.link(nc.vector.tensor_reduce(span1[:, :], spans[:, :], AX, ALU.max))
            ch(nc.vector.tensor_scalar(s.rounds[:, :], span1[:, :], WIN.bit_length() - 1, None, ALU.logical_shift_right))
            ch(nc.vector.memset(s.updT[:, :], 0.0))
            ve.wait_ge(mm_done, 1)
            ch.link(nc.vector.tensor_tensor(Mf[:, :, :], s.ps[2][0:NP, 0:NB * H0].rearrange("p (b j) -> p b j", j=H0),
                                            vr[:, 2 * D:].unsqueeze(1).to_broadcast([NP, NB, H0]), ALU.mult))
            ch.link(nc.vector.tensor_tensor(Mf[:, :, :], Mf[:, :, :],
                                            cmsg[:, :].unsqueeze(1).to_broadcast([NP, NB, H0]), ALU.add))
            ch.link(nc.vector.tensor_scalar(Mf[:, :, :], Mf[:, :, :], 0.0, None, ALU.max))
            ch.link(nc.vector.tensor_copy(Mt[:, :, 0:H0], Mf[:, :, :]))
            nc.vector.tensor_tensor(Mt[:, :, H0:], Mf[:, :, :], Mt[:, :, 0:H0].bitcast(F), ALU.subtract).then_inc(m_ready, 1)

        @block.tensor
        def _(pe):
            pe.wait_ge(pool, 4)
            pe.wait_ge(h_ready, 1)
            for k in range(2):
                for b in range(NB):
                    last = nc.tensor.transpose(s.ps[k][:, b * NP:(b + 1) * NP], s.h[:, b, k * P:(k + 1) * P], s.ident[0:NP, 0:NP])
                last.then_inc(hT_done, 1)
            pe.wait_ge(weights_in, 32)
            pe.wait_ge(hT_ready, 2)
            for b in range(NB):
                for k in range(2):
                    last = nc.tensor.matmul(s.ps[2][0:NP, b * H0:(b + 1) * H0], s.hT[:, k, b, :], w1[:, k, :],
                                            start=(k == 0), stop=(k == 1))
            last.then_inc(mm_done, 1)


def stage_edges0(nc, a, s, mtab):
    with ExitStack() as ctx:
        def sb(name, shape, dt=F):
            return ctx.enter_context(nc.sbuf_tensor(name, shape, dt))

        def sem(name):
            return ctx.enter_context(nc.semaphore(name))

        def two(f, name, *args):
            return [f(f"{name}{u}", *args) for u in range(2)]

        ea = two(sb, "ea", [P, A * P])
        idx = two(sb, "idx", [P, A], I32)
        mg = two(sb, "mg", [P, A, 2 * H0], FR)
        hb = two(sb, "hb", [P, A, KH])
        wh = two(sb, "wh", [P, A, KI])
        wp = two(sb, "wp", [P, 2, A, KI])
        mask = two(sb, "mask", [P, A, WIN])
        X = two(sb, "X", [P, A, 2, KI, WIN], FR)
        BT = sb("BT", [P, KI, CS])
        CT = sb("CT", [KI, CS])
        UT = sb("UT", [H0, CS])
        U = sb("U", [PC, NPC, H0])
        sel = two(sb, "sel", [PC, N])
        ea_in = two(sem, "ea_in")
        mg_in = [[sem(f"mg_in{u}{c}") for c in range(A)] for u in range(2)]
        idx_ready = sem("idx_ready")
        hid_done = sem("hid_done")
        hid_read = sem("hid_read")
        x_ready = sem("x_ready")
        bt_done = sem("bt_done")
        bt_kept = sem("bt_kept")
        dve = sem("dve_done0")
        ut_done = sem("ut_done")
        ut_kept = sem("ut_kept")
        u_done = sem("u_done")
        u_kept = sem("u_kept")
        sel_ready = sem("sel_ready")
        upd_done = sem("upd_done")
        round_done = sem("round_done")
        waited = sem("waited0")
        block = ctx.enter_context(nc.Block())
        CRED = 2
        hid_ps = [s.ps[6], s.ps[7]]

        def bt_ps(u, c):
            return s.ps[A * u + c]

        def rounds(eng):
            return eng.value_load(s.rounds[0:1, 0:1], min_val=0, max_val=ROUNDS - 1) + 1

        @block.sync
        def _(sp):
            with sp.Fori(0, rounds(sp)) as r:
                with sp.Fori(0, PAIRS) as t:
                    for u in range(2):
                        g = t * 2 + u
                        sp.wait_ge(hid_done, r * GR + g + 1)
                        sp.dma_start(ea[u][:, :], a["ea128T"][:, ds(g * (A * P), A * P)]).then_inc(ea_in[u], 16)

        @block.gpsimd
        def _(pl):
            with pl.Fori(0, rounds(pl)) as r:
                with pl.Fori(0, PAIRS) as t:
                    for u in range(2):
                        g = t * 2 + u
                        pl.wait_ge(bt_done, (r * GR + g) * A + A)
                        nc.gpsimd.tensor_copy(idx[u][:, :], s.src_i[:, ds(g * A, A)]).then_inc(idx_ready, 1)
                        pl.wait_ge(idx_ready, r * GR + g + 1)
                        pl.sem_inc(waited, 1)
                        for c in range(A):
                            pl.indirect_dma_start(mg[u][:, c, :].bitcast(F), None, mtab, bass.IndirectOffsetOnAxis(idx[u][:, c:c + 1], 0))\
                              .then_inc(mg_in[u][c], 16)

        @block.tensor
        def _(pe):
            pe.sem_inc(hid_done, CRED)
            pe.sem_inc(bt_done, CRED * A)

            def hid(r, t, u):
                g = t * 2 + u
                pe.wait_ge(ea_in[u], (r * PAIRS + t) * 16 + 16)
                pe.wait_ge(hid_read, r * GR + g + 1)
                for c in range(A):
                    last = nc.tensor.matmul(hid_ps[u][:, c * KH:(c + 1) * KH], ea[u][:, c * P:(c + 1) * P], s.kw1[:, :],
                                            start=True, stop=True)
                last.then_inc(hid_done, 1)

            def sums(r, t, u):
                g = t * 2 + u
                pe.wait_ge(bt_kept, r * GR + g + 1)
                for c in range(A):
                    pe.wait_ge(mg_in[u][c], (r * PAIRS + t) * 16 + 16)
                    pe.wait_ge(x_ready, (r * GR + g) * A + c + 1)
                    for part in range(2):
                        nc.tensor.matmul(bt_ps(u, c)[:, 0:XW], mg[u][:, c, :], X[u][:, c, part, :, :].rearrange("p i w -> p (i w)"),
                                         start=(part == 0), stop=(part == 1))
                    nc.tensor.matmul(bt_ps(u, c)[0:KI, XW:XW + WIN], wh[u][:, c, :], mask[u][:, c, :],
                                     start=True, stop=True).then_inc(bt_done, 1)

            with pe.Fori(0, rounds(pe)) as r:
                hid(r, 0, 0)
                with pe.Fori(0, PAIRS - 1) as t:
                    hid(r, t, 1)
                    sums(r, t, 0)
                    hid(r, t + 1, 0)
                    sums(r, t, 1)
                hid(r, PAIRS - 1, 1)
                sums(r, PAIRS - 1, 0)
                sums(r, PAIRS - 1, 1)
                pe.wait_ge(bt_kept, r * GR + GR + CRED)
                for i in range(KI):
                    for m in range(3):
                        nc.tensor.matmul(s.ps[m][0:H0, 0:THIRD], s.T[:, i, :], BT[:, i, m * THIRD:(m + 1) * THIRD],
                                         start=(i == 0), stop=False)
                for m in range(3):
                    last = nc.tensor.matmul(s.ps[m][0:H0, 0:THIRD], s.T0[:, :], CT[:, m * THIRD:(m + 1) * THIRD],
                                            start=False, stop=True)
                last.then_inc(ut_done, 1)
                pe.wait_ge(ut_kept, r + 1)
                pe.sem_inc(waited, 1)
                for j in range(NPC):
                    last = nc.tensor.transpose(s.ps[3 + j // 8][0:PC, (j % 8) * H0:(j % 8 + 1) * H0],
                                               UT[:, j:CS:NPC], s.ident[0:H0, 0:H0])
                last.then_inc(u_done, 1)
                pe.wait_ge(u_kept, r + 1)
                for j in range(NPC):
                    pe.wait_ge(sel_ready, r * NPC + j + 1)
                    nc.tensor.matmul(s.ps[5][0:H0, 0:N], U[:, j, :], sel[j % 2][:, :],
                                     start=(j == 0), stop=(j == NPC - 1)).then_inc(upd_done, 1)
                pe.wait_ge(round_done, r + 1)

        @block.scalar
        def _(act):
            act.sem_inc(bt_kept, CRED)
            with act.Fori(0, rounds(act)) as r:
                with act.Fori(0, PAIRS) as t:
                    for u in range(2):
                        g = t * 2 + u
                        for c in range(A):
                            act.wait_ge(bt_done, (r * GR + g) * A + (CRED * A + c + 1))
                            at = (g * A + c) * WIN
                            nc.scalar.activation(BT[:, :, ds(at, WIN)], bt_ps(u, c)[:, 0:XW].rearrange("p (i w) -> p i w", w=WIN), ACT.Copy)
                            last = nc.scalar.activation(CT[:, ds(at, WIN)], bt_ps(u, c)[0:KI, XW:XW + WIN], ACT.Copy)
                        last.then_inc(bt_kept, 1)
                act.wait_ge(ut_done, r + 1)
                for m in range(3):
                    last = nc.scalar.activation(UT[:, m * THIRD:(m + 1) * THIRD], s.ps[m][0:H0, 0:THIRD], ACT.Copy)
                last.then_inc(ut_kept, 1)
                act.wait_ge(u_done, r + 1)
                nc.scalar.activation(U[:, 0:8, :].rearrange("p a j -> p (a j)"), s.ps[3][0:PC, :], ACT.Copy)
                nc.scalar.activation(U[:, 8:NPC, :].rearrange("p a j -> p (a j)"), s.ps[4][0:PC, 0:(NPC - 8) * H0], ACT.Copy).then_inc(u_kept, 1)
                act.wait_ge(round_done, r + 1)

        @block.vector
        def _(ve):
            ve.sem_inc(hid_read, CRED)
            OPS = 5
            with ve.Fori(0, rounds(ve)) as r:
                with ve.Fori(0, PAIRS) as t:
                    for u in range(2):
                        g = t * 2 + u
                        done = (r * GR + g) * OPS
                        ve.wait_ge(bt_done, (r * GR + g) * A + A)
                        nc.vector.tensor_tensor(mask[u][:, :, :], s.dl[:, ds(g * A, A)].unsqueeze(2).to_broadcast([P, A, WIN]),
                                                s.iota_w[:, :].unsqueeze(1).to_broadcast([P, A, WIN]), ALU.is_equal).then_inc(dve, 1)
                        nc.vector.tensor_copy(wh[u][:, :, KH], s.w[:, ds(g * A, A)]).then_inc(dve, 1)
                        ve.wait_ge(hid_done, r * GR + g + (CRED + 1))
                        nc.vector.tensor_tensor(hb[u][:, :, :], hid_ps[u][:, 0:A * KH].rearrange("p (a i) -> p a i", a=A),
                                                s.kb1[:, :].unsqueeze(1).to_broadcast([P, A, KH]), ALU.add).then_inc(hid_read, 1)
                        ve.wait_ge(hid_read, r * GR + g + (CRED + 1))
                        nc.vector.scalar_tensor_tensor(wh[u][:, :, 0:KH], hb[u][:, :, :], 0.0,
                                                       s.w[:, ds(g * A, A)].unsqueeze(2).to_broadcast([P, A, KH]),
                                                       ALU.max, ALU.mult).then_inc(dve, 1)
                        ve.wait_ge(dve, done + 3)
                        nc.vector.tensor_copy(wp[u][:, 0, :, :].bitcast(FR), wh[u][:, :, :]).then_inc(dve, 1)
                        ve.wait_ge(dve, done + 4)
                        nc.vector.tensor_tensor(wp[u][:, 1, :, :].bitcast(FR), wh[u][:, :, :], wp[u][:, 0, :, :], ALU.subtract).then_inc(dve, 1)
                        ve.wait_ge(dve, done + OPS)
                        for c in range(A):
                            nc.vector.tensor_tensor(X[u][:, c, :, :, :], wp[u][:, :, c, :].unsqueeze(3).to_broadcast([P, 2, KI, WIN]),
                                                    mask[u][:, c, :].unsqueeze(1).unsqueeze(1).to_broadcast([P, 2, KI, WIN]),
                                                    ALU.mult).then_inc(x_ready, 1)
                for j in range(NPC):
                    if j >= 2:
                        ve.wait_ge(upd_done, r * NPC + j - 1)
                    nc.vector.tensor_scalar(sel[j % 2][:, :], s.iota_n[0:PC, :], s.node[:, j:j + 1], None, ALU.is_equal).then_inc(sel_ready, 1)
                ve.wait_ge(upd_done, r * NPC + NPC)
                ve.wait_ge(dve, (r * GR + GR) * OPS)
                ve.wait_ge(sel_ready, r * NPC + NPC)
                nc.vector.tensor_scalar(s.node[:, :], s.node[:, :], float(WIN), None, ALU.add)
                nc.vector.tensor_scalar(s.dl[:, :], s.dl[:, :], float(-WIN), None, ALU.add)
                nc.vector.tensor_tensor(s.updT[:, :], s.ps[5][0:H0, 0:N], s.updT[:, :], ALU.add).then_inc(round_done, 1)
                ve.wait_ge(round_done, r + 1)


def stage_nodes1(nc, a, s, ktab, vtab):
    with ExitStack() as ctx:
        def sb(name, shape, dt=F):
            return ctx.enter_context(nc.sbuf_tensor(name, shape, dt))

        def sem(name):
            return ctx.enter_context(nc.semaphore(name))

        s.mean = sb("mean1", [NP, NB])
        s.var = sb("var1", [NP, NB])
        s.rs = sb("rs1", [NP, NB])
        s.tmp4 = sb("tmp41", [NP, NB])
        s.h = sb("h1", [NP, NB, D])
        s.sq = sb("sq1", [NP, NB, D])
        s.hT = sb("hT1", [P, 2, NB, NP])
        vec = sb("vec1", [NP, len(VECS1), D])
        W = sb("Wqkv", [P, 2, 3, D])
        kb = sb("kb", [NP, D])
        kv = sb("kv", [NP, 2, NB, D])
        qf = sb("qf", [NP, NB, D])
        updR = sb("updR", [H0, N])
        w_in = sem("w_in")
        vec_in = sem("vec1_in")
        upd_ready = sem("upd_ready")
        out0_done = sem("out0_done")
        h_ready = sem("h1_ready")
        hT_done = sem("h1T_done")
        hT_ready = sem("h1T_ready")
        qkv_done = sem("qkv_done")
        kv_ready = sem("kv_ready")
        kv_out = sem("kv_out")
        dve = sem("dve_done1")
        sqrt_in = sem("sqrt1_in")
        sqrt_done = sem("sqrt1_done")
        block = ctx.enter_context(nc.Block())

        @block.sync
        def _(sp):
            sp.dma_start(vec[:, :, :].rearrange("p a d -> p (a d)"), a["vecs1"].to_broadcast([NP, len(VECS1) * D])).then_inc(vec_in, 16)
            for i, n in enumerate(("Wq", "Wk", "Wv")):
                sp.dma_start(W[:, :, i, :], a[n].rearrange("(k p) j -> p k j", p=P)).then_inc(w_in, 16)
            for i, tab in enumerate((ktab, vtab)):
                sp.wait_ge(kv_ready, i + 1)
                sp.dma_start(tab.rearrange("(b p) d -> p b d", p=NP), kv[:, i, :, :]).then_inc(kv_out, 16)
            sp.wait_ge(kv_out, 32)

        @block.scalar
        def _(act):
            act.activation(updR[:, :], s.updT[:, :], ACT.Relu, bias=s.upd_ab[:, 1:2], scale=s.upd_ab[:, 0:1]).then_inc(upd_ready, 1)
            act.wait_ge(sqrt_in, 1)
            act.activation(s.rs[:, :], s.var[:, :], ACT.Sqrt).then_inc(sqrt_done, 1)
            act.wait_ge(hT_done, 2)
            for k in range(2):
                act.activation(s.hT[:, k, :, :].rearrange("p b n -> p (b n)"), s.ps[2 + k][:, 0:N], ACT.Copy).then_inc(hT_ready, 1)

        @block.tensor
        def _(pe):
            pe.wait_ge(upd_ready, 1)
            for b in range(NB):
                last = nc.tensor.matmul(s.ps[b // 2][0:NP, (b % 2) * D:(b % 2 + 1) * D], updR[:, b * NP:(b + 1) * NP], s.w2s[:, :],
                                        start=True, stop=True)
            last.then_inc(out0_done, 1)
            pe.wait_ge(h_ready, 1)
            for k in range(2):
                for b in range(NB):
                    last = nc.tensor.transpose(s.ps[2 + k][:, b * NP:(b + 1) * NP], s.h[:, b, k * P:(k + 1) * P], s.ident[0:NP, 0:NP])
                last.then_inc(hT_done, 1)
            pe.wait_ge(hT_ready, 2)
            pe.wait_ge(w_in, 48)
            for i in range(3):
                for b in range(NB):
                    bank = s.ps[(4, 6, 0)[i] + b // 2]
                    for k in range(2):
                        last = nc.tensor.matmul(bank[0:NP, (b % 2) * D:(b % 2 + 1) * D], s.hT[:, k, b, :], W[:, k, i, :],
                                                start=(k == 0), stop=(k == 1))
                last.then_inc(qkv_done, 1)

        @block.vector
        def _(ve):
            ch = Chain(ve, dve)
            nv = {n: vec[:, i, :] for i, n in enumerate(VECS1)}
            ve.wait_ge(vec_in, 16)
            ch.link(nc.vector.tensor_tensor(kb[:, :], nv["bk"], nv["be"], ALU.add))
            ve.wait_ge(out0_done, 1)
            for b in range(2):
                ch(nc.vector.tensor_tensor(s.xres[:, 2 * b:2 * b + 2, :], s.ps[b][0:NP, :].rearrange("p (b d) -> p b d", b=2),
                                           s.xres[:, 2 * b:2 * b + 2, :], ALU.add))
            ch.wait()
            normalised(nc, ve, ch, sqrt_in, sqrt_done, (s.mean, s.var, s.rs, s.tmp4, s.sq), s.xres, s.h, 1, h_ready)
            ch.link(nc.vector.tensor_tensor(s.xres[:, :, :], s.xres[:, :, :], nv["bias"].unsqueeze(1).to_broadcast([NP, NB, D]), ALU.add))
            for i, (bias, to) in enumerate(((nv["bq"], qf[:, :, :]), (kb[:, :], kv[:, 0, :, :]), (nv["bv"], kv[:, 1, :, :]))):
                ve.wait_ge(qkv_done, i + 1)
                for b in range(2):
                    last = nc.vector.tensor_tensor(to[:, 2 * b:2 * b + 2, :], s.ps[(4, 6, 0)[i] + b][0:NP, :].rearrange("p (b d) -> p b d", b=2),
                                                   bias.unsqueeze(1).to_broadcast([NP, 2, D]), ALU.add)
                    if i:
                        if b:
                            last.then_inc(kv_ready, 1)
                    else:
                        ch(last)
                if i == 0:
                    ch.wait()
                    ch.link(nc.vector.tensor_copy(s.QT[:, :, 0, :], qf[:, :, :]))
                    ch.link(nc.vector.tensor_tensor(s.QT[:, :, 1, :], qf[:, :, :], s.QT[:, :, 0, :].bitcast(F), ALU.subtract))


def stage_scores(nc, a, s, ktab):
    with ExitStack() as ctx:
        def sb(name, shape, dt=F):
            return ctx.enter_context(nc.sbuf_tensor(name, shape, dt))

        def sem(name):
            return ctx.enter_context(nc.semaphore(name))

        def two(f, name, *args):
            return [f(f"{name}{u}", *args) for u in range(2)]

        We = sb("We", [P, D])
        Wp = sb("Wp", [P, 2, D], FR)
        ea = two(sb, "eb", [P, A * P])
        eh = two(sb, "eh", [P, A * P], FR)
        hi = two(sb, "ehi", [P, A * P])
        srcb = two(sb, "srcb", [NP, A * P], I32)
        oh = two(sb, "ohT", [NP, NB, A * P], FR)
        idx = two(sb, "idx1", [P, A], I32)
        kg = two(sb, "kg", [P, A, D])
        key = two(sb, "key", [P, A, D])
        pr = two(sb, "pr", [P, A, D])
        we_in = sem("we_in")
        ea_in = two(sem, "eb_in")
        src_in = two(sem, "srcb_in")
        kg_in = two(sem, "kg_in")
        idx_ready = sem("idx1_ready")
        hi_done = sem("hi_done")
        eh_ready = sem("eh_ready")
        oh_ready = sem("oh_ready")
        qe_done = sem("qe_done")
        qe_read = sem("qe_read")
        dve = sem("dve_done2")
        pool = sem("pool_done2")
        wp_ready = sem("wp_ready")
        alpha_done = sem("alpha_done")
        waited = sem("waited1")
        block = ctx.enter_context(nc.Block())
        CRED = 2

        def qe(u, c):
            return s.ps[A * u + c]

        @block.sync
        def _(sp):
            sp.dma_start(We[0:DE1, :], a["We"]).then_inc(we_in, 16)
            sp.dma_start(We[DE1:P, :], a["We"]).then_inc(we_in, 16)
            with sp.Fori(0, PAIRS) as t:
                for u in range(2):
                    g = t * 2 + u
                    sp.wait_ge(eh_ready, g + 1)
                    sp.wait_ge(hi_done, g + 1)
                    for part in range(2):
                        sp.dma_start(ea[u][part * DE1:(part + 1) * DE1, :], a["ea64T"][:, ds(g * (A * P), A * P)]).then_inc(ea_in[u], 16)
                    sp.wait_ge(oh_ready, g + 1)
                    sp.dma_start(srcb[u][:, :], a["src_row"][:, ds(g * (A * P), A * P)].to_broadcast([NP, A * P])).then_inc(src_in[u], 16)

        @block.gpsimd
        def _(pl):
            nc.gpsimd.iota(s.nodeid[:, :], pattern=[[NP, NB]], base=0, channel_multiplier=1,
                           allow_small_or_imprecise_dtypes=True).then_inc(pool, 1)
            with pl.Fori(0, PAIRS) as t:
                for u in range(2):
                    g = t * 2 + u
                    pl.wait_ge(dve, g * 1 + 1)
                    nc.gpsimd.tensor_copy(idx[u][:, :], s.dst_i[:, ds(g * A, A)]).then_inc(idx_ready, 1)
                    pl.wait_ge(idx_ready, g + 1)
                    pl.sem_inc(waited, 1)
                    for c in range(A):
                        pl.indirect_dma_start(kg[u][:, c, :], None, ktab, bass.IndirectOffsetOnAxis(idx[u][:, c:c + 1], 0))\
                          .then_inc(kg_in[u], 16)

        @block.scalar
        def _(act):
            act.sem_inc(hi_done, CRED)
            with act.Fori(0, PAIRS) as t:
                for u in range(2):
                    g = t * 2 + u
                    act.wait_ge(ea_in[u], t * 32 + 32)
                    act.wait_ge(qe_done, g + 1)
                    act.wait_ge(eh_ready, g + 1)
                    nc.scalar.activation(eh[u][0:DE1, :], ea[u][0:DE1, :], ACT.Copy)
                    nc.scalar.activation(hi[u][DE1:P, :].bitcast(FR), ea[u][DE1:P, :], ACT.Copy).then_inc(hi_done, 1)

        @block.tensor
        def _(pe):
            pe.sem_inc(qe_done, CRED)
            pe.wait_ge(wp_ready, 1)
            with pe.Fori(0, PAIRS) as t:
                for u in range(2):
                    g = t * 2 + u
                    pe.wait_ge(hi_done, g + (CRED + 1))
                    pe.wait_ge(eh_ready, g + (CRED + 1))
                    pe.wait_ge(oh_ready, g + (CRED + 1))
                    pe.wait_ge(qe_read, g + 1)
                    for c in range(A):
                        for part in range(2):
                            nc.tensor.matmul(qe(u, c)[:, D:2 * D], eh[u][:, c * P:(c + 1) * P], Wp[:, part, :],
                                             start=(part == 0), stop=(part == 1))
                        for b in range(NB):
                            for part in range(2):
                                last = nc.tensor.matmul(qe(u, c)[:, 0:D], oh[u][:, b, c * P:(c + 1) * P], s.QT[:, b, part, :],
                                                        start=(b == 0 and part == 0), stop=(b == NB - 1 and part == 1))
                    last.then_inc(qe_done, 1)

        @block.vector
        def _(ve):
            ve.sem_inc(eh_ready, CRED)
            ve.sem_inc(oh_ready, CRED)
            ve.sem_inc(qe_read, CRED)
            ve.sem_inc(dve, CRED)
            ve.wait_ge(we_in, 32)
            nc.vector.tensor_copy(Wp[:, 0, :], We[:, :]).then_inc(pool, 1)
            ve.wait_ge(pool, 2)
            nc.vector.tensor_tensor(Wp[:, 1, :], We[:, :], Wp[:, 0, :].bitcast(F), ALU.subtract).then_inc(wp_ready, 1)

            def prepare(t, u):
                g = t * 2 + u
                ve.wait_ge(hi_done, g + (CRED + 1))
                nc.vector.tensor_tensor(eh[u][DE1:P, :], ea[u][DE1:P, :], hi[u][DE1:P, :], ALU.subtract).then_inc(eh_ready, 1)
                ve.wait_ge(src_in[u], t * 16 + 16)
                ve.wait_ge(qe_done, g + 1)
                for b in range(NB):
                    last = nc.vector.tensor_scalar(oh[u][:, b, :], srcb[u][:, :], s.nodeid[:, b:b + 1], None, ALU.is_equal)
                last.then_inc(oh_ready, 1)

            def scores(t, u):
                g = t * 2 + u
                ve.wait_ge(kg_in[u], t * (16 * A) + 16 * A)
                ve.wait_ge(qe_done, g + (CRED + 1))
                banks = s.banks3(u)
                nc.vector.tensor_tensor(key[u][:, :, :], banks[:, :, D:2 * D], kg[u][:, :, :], ALU.add).then_inc(dve, 1)
                ve.wait_ge(dve, g + (CRED + 1))
                nc.vector.tensor_tensor(pr[u][:, :, :], banks[:, :, 0:D], key[u][:, :, :], ALU.mult).then_inc(qe_read, 1)
                ve.wait_ge(qe_read, g + (CRED + 1))
                nc.vector.tensor_reduce(s.alpha[:, ds(g * A, A), :].rearrange("p a h -> p (a h)"),
                                        pr[u][:, :, :].rearrange("p a (h c) -> p (a h) c", c=C), AX, ALU.add).then_inc(alpha_done, 1)
                ve.wait_ge(alpha_done, g + 1)

            prepare(0, 0)
            with ve.Fori(0, PAIRS - 1) as t:
                prepare(t, 1)
                scores(t, 0)
                prepare(t + 1, 0)
                scores(t, 1)
            prepare(PAIRS - 1, 1)
            scores(PAIRS - 1, 0)
            scores(PAIRS - 1, 1)


def stage_softmax(nc, a, s):
    with ExitStack() as ctx:
        def sb(name, shape, dt=F):
            return ctx.enter_context(nc.sbuf_tensor(name, shape, dt))

        def sem(name):
            return ctx.enter_context(nc.semaphore(name))

        pm = sb("pm", [P, HEADS])
        am = sb("am", [P, HEADS])
        sm = sb("sm", [P, HEADS])
        masked = sem("masked")
        pm_ready = sem("pm_ready")
        am_ready = sem("am_ready")
        shifted = sem("shifted")
        exp_done = sem("exp_done")
        sm_ready = sem("sm_ready")
        total_ready = sem("total_ready")
        rsum_ready = sem("rsum_ready")
        block = ctx.enter_context(nc.Block())
        by_head = s.alpha[:, :, :].rearrange("p c h -> p h c")
        first = E // P

        @block.gpsimd
        def _(pl):
            part = s.alpha[:, first:, :]
            nc.gpsimd.affine_select(out=part, in_=part, compare_op=ALU.is_ge, fill=-3.0e38, base=E - 1 - first * P,
                                    pattern=[[-P, CH - first], [0, HEADS]], channel_multiplier=-1).then_inc(masked, 1)
            pl.wait_ge(pm_ready, 1)
            nc.gpsimd.partition_all_reduce(am[:, :], pm[:, :], P, bass.bass_isa.ReduceOp.max).then_inc(am_ready, 1)
            pl.wait_ge(sm_ready, 1)
            nc.gpsimd.partition_all_reduce(pm[:, :], sm[:, :], P, bass.bass_isa.ReduceOp.add).then_inc(total_ready, 1)

        @block.vector
        def _(ve):
            ve.wait_ge(masked, 1)
            nc.vector.tensor_reduce(pm[:, :], by_head, AX, ALU.max).then_inc(pm_ready, 1)
            ve.wait_ge(am_ready, 1)
            nc.vector.tensor_tensor(s.alpha[:, :, :], s.alpha[:, :, :], am[:, :].unsqueeze(1).to_broadcast([P, CH, HEADS]),
                                    ALU.subtract).then_inc(shifted, 1)
            ve.wait_ge(exp_done, 1)
            nc.vector.tensor_reduce(sm[:, :], by_head, AX, ALU.add).then_inc(sm_ready, 1)
            ve.wait_ge(total_ready, 1)
            nc.vector.reciprocal(s.rsum[:, :], pm[:, :]).then_inc(rsum_ready, 1)

        @block.scalar
        def _(act):
            act.wait_ge(shifted, 1)
            act.activation(s.alpha[:, :, :], s.alpha[:, :, :], ACT.Exp, scale=float(C) ** -0.5).then_inc(exp_done, 1)


def stage_values(nc, a, s, vtab, out):
    with ExitStack() as ctx:
        def sb(name, shape, dt=F):
            return ctx.enter_context(nc.sbuf_tensor(name, shape, dt))

        def sem(name):
            return ctx.enter_context(nc.semaphore(name))

        def two(f, name, *args):
            return [f(f"{name}{u}", *args) for u in range(2)]

        idx = two(sb, "idx2", [P, A], I32)
        vg = two(sb, "vg", [P, A, D])
        pv = two(sb, "pv", [P, A, D])
        ph = two(sb, "ph", [P, A, D], FR)
        pl_ = two(sb, "pl", [P, A, D], FR)
        oh = two(sb, "oh", [P, A, N], FR)
        zero = sb("zero", [P, D])
        scaled = sb("scaled", [NP, NB, D])
        res = sb("res", [NP, NB, D])
        vg_in = two(sem, "vg_in")
        idx_ready = sem("idx2_ready")
        vg_read = sem("vg_read")
        ph_ready = sem("ph_ready")
        pl_ready = sem("pl_ready")
        oh_ready = sem("oh2_ready")
        sum_done = sem("sum_done")
        all_done = sem("all_done")
        zero_ready = sem("zero_ready")
        dve = sem("dve_done4")
        res_ready = sem("res_ready")
        res_out = sem("res_out")
        waited = sem("waited2")
        block = ctx.enter_context(nc.Block())
        CRED = 2

        @block.sync
        def _(sp):
            sp.wait_ge(res_ready, 1)
            sp.dma_start(out.rearrange("(b p) d -> p b d", p=NP), res[:, :, :]).then_inc(res_out, 16)
            sp.wait_ge(res_out, 16)

        @block.gpsimd
        def _(pl):
            with pl.Fori(0, PAIRS) as t:
                for u in range(2):
                    g = t * 2 + u
                    pl.wait_ge(vg_read, g + 1)
                    nc.gpsimd.tensor_copy(idx[u][:, :], s.dst_i[:, ds(g * A, A)]).then_inc(idx_ready, 1)
                    pl.wait_ge(idx_ready, g + 1)
                    pl.sem_inc(waited, 1)
                    for c in range(A):
                        pl.indirect_dma_start(vg[u][:, c, :], None, vtab, bass.IndirectOffsetOnAxis(idx[u][:, c:c + 1], 0))\
                          .then_inc(vg_in[u], 16)

        @block.scalar
        def _(act):
            act.sem_inc(ph_ready, CRED)
            with act.Fori(0, PAIRS) as t:
                for u in range(2):
                    g = t * 2 + u
                    act.wait_ge(vg_read, g + (CRED + 1))
                    act.wait_ge(pl_ready, g + 1)
                    act.wait_ge(sum_done, g + 1)
                    nc.scalar.activation(ph[u][:, :, :], pv[u][:, :, :], ACT.Copy).then_inc(ph_ready, 1)

        @block.tensor
        def _(pe):
            pe.sem_inc(sum_done, CRED)
            pe.wait_ge(zero_ready, 1)
            for b in range(NB):
                nc.tensor.matmul(s.ps[b][0:NP, 0:D], zero[:, 0:NP], zero[:, :], start=True, stop=False)
            with pe.Fori(0, PAIRS) as t:
                for u in range(2):
                    g = t * 2 + u
                    pe.wait_ge(oh_ready, g + 1)
                    pe.wait_ge(ph_ready, g + (CRED + 1))
                    pe.wait_ge(pl_ready, g + (CRED + 1))
                    for c in range(A):
                        for b in range(NB):
                            for part in (ph, pl_):
                                last = nc.tensor.matmul(s.ps[b][0:NP, 0:D], oh[u][:, c, b * NP:(b + 1) * NP], part[u][:, c, :],
                                                        start=False, stop=False)
                    last.then_inc(sum_done, 1)
            for b in range(NB):
                last = nc.tensor.matmul(s.ps[b][0:NP, 0:D], zero[:, 0:NP], zero[:, :], start=False, stop=True)
            last.then_inc(all_done, 1)

        @block.vector
        def _(ve):
            ve.sem_inc(vg_read, CRED)
            ve.sem_inc(pl_ready, CRED)
            nc.vector.memset(zero[:, :], 0.0).then_inc(zero_ready, 1)

            def weigh(t, u):
                g = t * 2 + u
                ve.wait_ge(vg_in[u], t * (16 * A) + 16 * A)
                ve.wait_ge(ph_ready, g + 1)
                ve.wait_ge(pl_ready, g + 1)
                nc.vector.tensor_tensor(pv[u][:, :, :].rearrange("p a (h c) -> p (a h) c", c=C),
                                        vg[u][:, :, :].rearrange("p a (h c) -> p (a h) c", c=C),
                                        s.alpha[:, ds(g * A, A), :].rearrange("p a h -> p (a h)").unsqueeze(2).to_broadcast([P, A * HEADS, C]),
                                        ALU.mult).then_inc(vg_read, 1)
                ve.wait_ge(sum_done, g + 1)
                for c in range(A):
                    last = nc.vector.tensor_scalar(oh[u][:, c, :], s.iota_n[:, :], s.src_f[:, ds(g * A + c, 1)], None, ALU.is_equal)
                last.then_inc(oh_ready, 1)

            def low(t, u):
                g = t * 2 + u
                ve.wait_ge(ph_ready, g + (CRED + 1))
                nc.vector.tensor_tensor(pl_[u][:, :, :], pv[u][:, :, :], ph[u][:, :, :].bitcast(F), ALU.subtract).then_inc(pl_ready, 1)

            with ve.Fori(0, PAIRS) as t:
                for u in range(2):
                    weigh(t, u)
                    low(t, u)
            ve.wait_ge(all_done, 1)
            for b in range(NB):
                last = nc.vector.tensor_tensor(scaled[:, b, :].rearrange("p (h c) -> p h c", c=C),
                                               s.ps[b][0:NP, 0:D].rearrange("p (h c) -> p h c", c=C),
                                               s.rsum[0:NP, :].unsqueeze(2).to_broadcast([NP, HEADS, C]), ALU.mult)
            last.then_inc(dve, 1)
            ve.wait_ge(dve, 1)
            nc.vector.tensor_tensor(res[:, :, :], scaled[:, :, :], s.xres[:, :, :], ALU.add).then_inc(res_ready, 1)


def kernel(**inputs):
    import numpy as np
    import concourse.bacc as bacc
    from concourse.bass_utils import run_bass_kernel_spmd

    x = {k: np.ascontiguousarray(v) for k, v in inputs.items()}
    l0 = {k[7:]: v for k, v in x.items() if k.startswith("L0_gnn_")}
    l1 = {k[7:]: v for k, v in x.items() if k.startswith("L1_gnn_")}

    def padded(v, fill):
        return np.pad(v, [(0, 0)] * (v.ndim - 1) + [(0, EP - E)], constant_values=fill)

    def per_chunk(v):
        return np.ascontiguousarray(v.reshape(CH, P).T)

    src, dst = padded(x["src"], 0), padded(x["dst"], N - 1)
    kw2 = l0["kw2"].reshape(KH, H0 + 1, H0)
    kb2 = l0["kb2"].reshape(1, H0 + 1, H0)
    rows = np.concatenate([kw2, kb2])
    arrays = {
        "x": x["x"],
        "src_pc": per_chunk(src),
        "dst_pc": per_chunk(dst),
        "src_row": src.reshape(1, EP),
        "dst_rows": dst.reshape(GR, A, P),
        "w_pc": per_chunk(padded(x["edge_weight"], 0)),
        "ea128T": np.ascontiguousarray(padded(x["edge_attr_128"].T, 0)),
        "ea64T": np.ascontiguousarray(padded(x["edge_attr_64"].T, 0)),
        "vecs0": np.concatenate([l0[n] for n in VECS0]).reshape(1, -1),
        "vecs1": np.concatenate([l1[n] for n in VECS1]).reshape(1, -1),
        "msg_vecs": np.concatenate([l0[n] for n in ("g_msg", "be_msg", "m_msg", "v_msg", "b1")]).reshape(1, -1),
        "upd_vecs": np.ascontiguousarray(np.stack([l0[n] for n in ("g_upd", "be_upd", "m_upd", "v_upd")], axis=1)),
        "w1": l0["w1"], "w2": l0["w2"], "kw1": l0["kw1"], "kb1": l0["kb1"].reshape(1, KH),
        "T": np.ascontiguousarray(rows[:, 1:, :].transpose(2, 0, 1)),
        "T0": np.ascontiguousarray(rows[:, 0, :]),
        "Wq": l1["Wq"], "Wk": l1["Wk"], "Wv": l1["Wv"], "We": l1["We"],
    }
    nc = bacc.Bacc("TRN2", target_bir_lowering=False, num_devices=1)
    aps = {n: nc.dram_tensor(f"in_{n}", v.shape, mybir.dt.from_np(v.dtype), kind="ExternalInput").ap() for n, v in arrays.items()}
    out = nc.dram_tensor("out", [N, D], F, kind="ExternalOutput").ap()
    build(nc, aps, out)
    r = run_bass_kernel_spmd(nc, [{f"in_{n}": v for n, v in arrays.items()}], core_ids=[0])
    return r.results[0]["out"]
```

```python
import concourse.bass as bass
from concourse import mybir
from contextlib import ExitStack


N, E = 500, 16500
D, DE0, DE1 = 256, 128, 64
H0, KH = 64, 32
HEADS, C = 8, 32
EPS = 1e-5
P = 128
NB, NP = 4, 125
A = 2
STEPS = -(-E // (P * A * 2))
GR = 2 * STEPS
CH = GR * A
EP = CH * P
GE = A * P
BUF1 = 6
STEPS1 = GR // BUF1
PAIRS = BUF1 // 2
BANKS = 3
WIN = 6
WIN1 = 16
R1 = 2 * WIN1
KI = KH + 1
BUF0 = 3
STEPS0 = GR // BUF0
SEGS = 2
SEG = STEPS0 // SEGS
IPS = KI // SEG
XW = KI * WIN
CS = CH * WIN
ROUNDS = -(-N // WIN)
SC = CS // SEGS
PC = 99
NPC = CS // PC
VECS0 = ["g_in", "be_in", "m_in", "v_in", "g_out", "be_out", "m_out", "v_out", "b2"]
VECS1 = ["bq", "bk", "bv", "be", "bias"]
assert N == NB * NP and SC <= 512 and CS % PC == 0 and SEG * SEGS == STEPS0 and BUF0 * STEPS0 == GR and IPS * SEG == KI and A * (XW + WIN) <= 512

F = mybir.dt.float32
FR = mybir.dt.float32r
I32 = mybir.dt.int32
ALU = mybir.AluOpType
ACT = mybir.ActivationFunctionType
AX = mybir.AxisListType.X


class Chain:

    def __init__(self, eng, sem):
        self.eng, self.sem, self.n = eng, sem, 0

    def __call__(self, ins):
        self.n += 1
        ins.then_inc(self.sem, 1)
        return ins

    def wait(self):
        self.eng.wait_ge(self.sem, self.n)

    def link(self, ins):
        self(ins)
        self.wait()


def ds(start, size):
    return bass.ds(start, size)


def normalised(nc, eng, ch, sqrt_in, sqrt_done, tiles, xin, hout, n, ready=None):
    mean, var, rs, tmp, sq = tiles
    ch.link(nc.vector.tensor_reduce(mean[:, :], xin[:, :, :], AX, ALU.add))
    ch.link(nc.vector.tensor_scalar(mean[:, :], mean[:, :], 1.0 / D, None, ALU.mult))
    ch.link(nc.vector.tensor_tensor(hout[:, :, :], xin[:, :, :], mean[:, :].unsqueeze(2).to_broadcast([NP, NB, D]), ALU.subtract))
    ch.link(nc.vector.tensor_tensor(sq[:, :, :], hout[:, :, :], hout[:, :, :], ALU.mult))
    ch.link(nc.vector.tensor_reduce(var[:, :], sq[:, :, :], AX, ALU.add))
    nc.vector.tensor_scalar(var[:, :], var[:, :], 1.0 / D, EPS, ALU.mult, ALU.add).then_inc(sqrt_in, 1)
    eng.wait_ge(sqrt_done, n)
    rsqrt_refined(nc, ch, rs[:, :], var[:, :], tmp[:, :])
    ch.link(nc.vector.tensor_tensor(hout[:, :, :], hout[:, :, :], rs[:, :].unsqueeze(2).to_broadcast([NP, NB, D]), ALU.mult))
    last = nc.vector.tensor_scalar(hout[:, :, :], hout[:, :, :], 0.0, None, ALU.max)
    if ready is None:
        ch.link(last)
    else:
        last.then_inc(ready, 1)


def rsqrt_refined(nc, ch, rs, v, tmp):
    ch.wait()
    ch.link(nc.vector.reciprocal(rs, rs))
    ch.link(nc.vector.tensor_tensor(tmp, rs, rs, ALU.mult))
    ch.link(nc.vector.tensor_tensor(tmp, tmp, v, ALU.mult))
    ch.link(nc.vector.tensor_scalar(tmp, tmp, -0.5, 1.5, ALU.mult, ALU.add))
    ch.link(nc.vector.tensor_tensor(rs, rs, tmp, ALU.mult))


def build(nc, a, out):
    mtab = nc.dram_tensor("mtab", [N, 2 * H0], F, kind="Internal").ap()
    qtab = nc.dram_tensor("qtab", [N, D], F, kind="Internal").ap()
    ktab = nc.dram_tensor("ktab", [N + WIN1, 2 * D], F, kind="Internal").ap()
    vtab = nc.dram_tensor("vtab", [N + WIN1, 2 * D], F, kind="Internal").ap()
    eh_d = nc.dram_tensor("eh_d", [P, GR, GE], F, kind="Internal").ap()
    src_d = nc.dram_tensor("src_d", [EP], F, kind="Internal").ap()
    dst_d = nc.dram_tensor("dst_d", [EP], F, kind="Internal").ap()
    lo_i_d = nc.dram_tensor("lo_i_d", [CH], I32, kind="Internal").ap()
    lo_d = nc.dram_tensor("lo_d", [CH], F, kind="Internal").ap()
    span_d = nc.dram_tensor("span_d", [CH], F, kind="Internal").ap()
    node_d = nc.dram_tensor("node_d", [CS], F, kind="Internal").ap()
    ctx = ExitStack()
    with ctx:
        def sb(name, shape, dt=F, c=ctx):
            return c.enter_context(nc.sbuf_tensor(name, shape, dt))

        class Shared:
            pass

        s = Shared()
        psum = ctx.enter_context(nc.psum_tensor("psum", [P, 8, 512], F))
        s.psum = psum
        s.ps = [psum[:, i, :] for i in range(8)]
        s.ident = sb("ident", [P, P])
        s.xres = sb("xres", [NP, NB, D])
        s.src_i = sb("src_i", [P, CH], I32)
        s.src_f = sb("src_f", [P, CH])
        s.w = sb("w", [P, CH])
        s.dl = sb("dl", [P, CH])
        s.rounds = sb("rounds", [1, 1], I32)
        s.rounds1 = sb("rounds1", [1, 1], I32)
        s.lo_i = sb("lo_i", [1, CH], I32)
        s.start = sb("start", [1, CH], I32)
        s.node = sb("node", [PC, NPC])
        s.wn = sb("wn", [P, STEPS])
        s.wn0 = sb("wn0", [P, STEPS])
        s.iota_n = sb("iota_n", [P, N])
        s.iota_w = sb("iota_w", [P, WIN])
        s.nodeid = sb("nodeid", [NP, NB])
        s.updT = sb("updT", [H0, N])
        s.w2s = sb("w2s", [H0, D])
        s.upd_ab = sb("upd_ab", [H0, 2])
        s.kb1 = sb("kb1", [KH, 1])
        s.kw1 = sb("kw1", [P, KH])
        s.T = sb("T", [P, KI, H0])
        s.T0 = sb("T0", [KI, H0])
        stage_nodes0(nc, a, s, mtab, lo_d, lo_i_d, span_d, node_d, src_d, dst_d, ktab, vtab)
        stage_edges0(nc, a, s, mtab, eh_d)
        s.QT = sb("QT", [NP, NB, 2, D], FR)
        stage_nodes1(nc, a, s, qtab, ktab, vtab)
        s.alpha = sb("alpha", [P, CH, HEADS])
        s.dstb = sb("dstb", [P, STEPS, P])
        stage_scores(nc, a, s, qtab, ktab, eh_d, src_d, dst_d)
        s.rsum = sb("rsum", [P, HEADS])
        stage_softmax(nc, a, s)
        stage_values(nc, a, s, vtab, out)


def stage_nodes0(nc, a, s, mtab, lo_d, lo_i_d, span_d, node_d, src_d, dst_d, ktab, vtab):
    with ExitStack() as ctx:
        def sb(name, shape, dt=F):
            return ctx.enter_context(nc.sbuf_tensor(name, shape, dt))

        def sem(name):
            return ctx.enter_context(nc.semaphore(name))

        s.mean = sb("mean0", [NP, NB])
        s.var = sb("var0", [NP, NB])
        s.rs = sb("rs0", [NP, NB])
        s.tmp4 = sb("tmp40", [NP, NB])
        s.h = sb("h0", [NP, NB, D])
        s.sq = sb("sq0", [NP, NB, D])
        s.hT = sb("hT0", [P, 2, NB, NP])
        vec = sb("vec0", [NP, len(VECS0), D])
        small = sb("small", [NP, 5, H0])
        vr = sb("vr", [NP, 2 * D + H0])
        vv = sb("vv", [NP, 2 * D + H0])
        vt = sb("vt", [NP, 2 * D + H0])
        cin = sb("cin", [NP, D])
        cmsg = sb("cmsg", [NP, H0])
        w1 = sb("w1", [P, 2, H0])
        ones1 = sb("ones1", [1, P])
        up = sb("up", [H0, 4])
        upt = sb("upt", [H0, 4])
        Mf = sb("Mf", [NP, NB, H0])
        Mt = sb("Mt", [NP, NB, 2 * H0], FR)
        C4 = 2 * A
        dr = sb("dr", [STEPS, C4, P], I32)
        sr = sb("sr", [STEPS, C4, P], I32)
        drf = sb("drf", [STEPS, C4, P])
        srf = sb("srf", [STEPS, C4, P])
        lo = sb("lo", [STEPS, C4])
        lo_i = sb("lo_ii", [STEPS, C4], I32)
        lox = sb("lox", [STEPS, C4, R1])
        hi = sb("hi", [STEPS, C4])
        span = sb("span", [STEPS, C4])
        nodes = sb("nodes", [STEPS, C4, WIN])
        lob = sb("lob", [P, CH])
        dst_i = sb("dst_i", [P, CH], I32)
        spans = sb("spans", [1, CH])
        span1 = sb("span1", [1, 1])
        over = sb("over", [1, ROUNDS])
        count = sb("count", [1, 1])
        slot_i = sb("slot_i", [P, 1], I32)
        slot = sb("slot", [P, 1])
        zero = sb("zero_rows", [WIN1, 2 * D])
        lox_ready = sem("lox_ready")
        wn_done = sem("wn_done")
        rows_ready = sem("rows_ready")
        rows_out = sem("rows_out")
        x_in = sem("x_in")
        vec_in = sem("vec_in")
        dst_in = sem("dst_in")
        weights_in = sem("weights_in")
        edge_in = sem("edge_in")
        win_out = sem("win_out")
        win_in = sem("win_in")
        win_ready = sem("win_ready")
        m_out = sem("m_out")
        m_ready = sem("m_ready")
        dve = sem("dve_done")
        pool = sem("pool_done")
        sqrt_in = sem("sqrt_in")
        sqrt_done = sem("sqrt_done")
        h_ready = sem("h_ready")
        hT_done = sem("hT_done")
        hT_ready = sem("hT_ready")
        mm_done = sem("mm_done")
        block = ctx.enter_context(nc.Block())

        @block.sync
        def _(sp):
            sp.dma_start(s.h[:, :, :], a["x"].rearrange("(b p) d -> p b d", p=NP)).then_inc(x_in, 16)
            sp.dma_start(vec[:, :, :].rearrange("p a d -> p (a d)"), a["vecs0"].to_broadcast([NP, len(VECS0) * D])).then_inc(vec_in, 16)
            sp.dma_start(small[:, :, :].rearrange("p a d -> p (a d)"), a["msg_vecs"].to_broadcast([NP, 5 * H0])).then_inc(vec_in, 16)
            sp.dma_start(up[:, :], a["upd_vecs"]).then_inc(vec_in, 16)
            sp.dma_start(w1[:, :, :], a["w1"].rearrange("(k p) j -> p k j", p=P)).then_inc(weights_in, 16)
            sp.dma_start(s.w2s[:, :], a["w2"]).then_inc(weights_in, 16)
            sp.dma_start(s.w[:, :], a["w_pc"]).then_inc(edge_in, 16)
            sp.wait_ge(rows_ready, 1)
            sp.dma_start(dst_d.rearrange("(g a) -> g a", a=C4 * P), drf[:, :, :].rearrange("g a e -> g (a e)")).then_inc(rows_out, 16)
            sp.dma_start(src_d.rearrange("(g a) -> g a", a=C4 * P), srf[:, :, :].rearrange("g a e -> g (a e)")).then_inc(rows_out, 16)
            sp.dma_start(ktab[N:, :], zero[:, :]).then_inc(rows_out, 16)
            sp.dma_start(vtab[N:, :], zero[:, :]).then_inc(rows_out, 16)
            sp.wait_ge(rows_out, 64)
            sp.wait_ge(m_ready, 1)
            sp.dma_start(mtab.rearrange("(b p) d -> p b d", p=NP), Mt[:, :, :].bitcast(F)).then_inc(m_out, 16)
            sp.wait_ge(m_out, 16)

        @block.scalar
        def _(act):
            act.dma_start(dr[:, :, :], a["dst_rows"]).then_inc(dst_in, 16)
            act.dma_start(sr[:, :, :], a["src_rows"]).then_inc(dst_in, 16)
            act.dma_start(s.src_i[:, :], a["src_pc"]).then_inc(edge_in, 16)
            act.dma_start(dst_i[:, :], a["dst_pc"]).then_inc(edge_in, 16)
            act.dma_start(s.kw1[:, :], a["kw1"]).then_inc(edge_in, 16)
            act.dma_start(s.kb1[:, :], a["kb1"]).then_inc(edge_in, 16)
            act.dma_start(s.T[0:H0, :, :], a["T"]).then_inc(edge_in, 16)
            act.dma_start(s.T[H0:P, :, :], a["T"]).then_inc(edge_in, 16)
            act.dma_start(s.T0[:, :], a["T0"]).then_inc(edge_in, 16)
            act.wait_ge(win_ready, 1)
            act.dma_start(lo_d.rearrange("(g a) -> g a", a=C4), lo[:, :]).then_inc(win_out, 16)
            act.dma_start(lo_i_d.rearrange("(g a) -> g a", a=C4), lo_i[:, :]).then_inc(win_out, 16)
            act.dma_start(span_d.rearrange("(g a) -> g a", a=C4), span[:, :]).then_inc(win_out, 16)
            act.dma_start(node_d.rearrange("(g a) -> g a", a=C4 * WIN), nodes[:, :, :].rearrange("g a w -> g (a w)")).then_inc(win_out, 16)
            act.wait_ge(win_out, 64)
            act.dma_start(lob[:, :], lo_d.rearrange("(o c) -> o c", o=1).to_broadcast([P, CH])).then_inc(win_in, 16)
            act.dma_start(s.lo_i[:, :], lo_i_d.rearrange("(o c) -> o c", o=1)).then_inc(win_in, 16)
            act.dma_start(spans[:, :], span_d.rearrange("(o c) -> o c", o=1)).then_inc(win_in, 16)
            act.dma_start(s.node[:, :], node_d.rearrange("(q j) -> q j", j=NPC)).then_inc(win_in, 16)
            act.wait_ge(sqrt_in, 1)
            act.activation(vr[:, :], vv[:, :], ACT.Sqrt).then_inc(sqrt_done, 1)
            act.activation(upt[:, 0:1], upt[:, 1:2], ACT.Sqrt).then_inc(sqrt_done, 1)
            act.wait_ge(sqrt_in, 2)
            act.activation(s.rs[:, :], s.var[:, :], ACT.Sqrt).then_inc(sqrt_done, 1)
            act.wait_ge(hT_done, 2)
            for k in range(2):
                act.activation(s.hT[:, k, :, :].rearrange("p b n -> p (b n)"), s.ps[k][:, 0:N], ACT.Copy).then_inc(hT_ready, 1)

        @block.gpsimd
        def _(pl):
            ch = Chain(pl, pool)
            ch(nc.gpsimd.memset(s.ident[:, :], 0.0))
            ch(nc.gpsimd.iota(s.iota_n[:, :], pattern=[[1, N]], base=0, channel_multiplier=0, allow_small_or_imprecise_dtypes=True))
            ch(nc.gpsimd.iota(s.iota_w[:, :], pattern=[[1, WIN]], base=0, channel_multiplier=0, allow_small_or_imprecise_dtypes=True))
            ch(nc.gpsimd.iota(s.nodeid[:, :], pattern=[[NP, NB]], base=0, channel_multiplier=1, allow_small_or_imprecise_dtypes=True))
            ch(nc.gpsimd.iota(slot_i[:, :], pattern=[[0, 1]], base=0, channel_multiplier=1))
            ch(nc.gpsimd.memset(zero[:, :], 0.0))
            ch.wait()
            ch(nc.gpsimd.affine_select(out=s.ident[:, :], in_=s.ident[:, :], compare_op=ALU.not_equal, fill=1.0,
                                       base=0, pattern=[[-1, P]], channel_multiplier=1))

        @block.vector
        def _(ve):
            ch = Chain(ve, dve)
            nv = {n: vec[:, i, :] for i, n in enumerate(VECS0)}
            ve.wait_ge(dst_in, 32)
            ve.wait_ge(pool, 6)
            ch(nc.vector.tensor_copy(drf[:, :, :], dr[:, :, :]))
            nc.vector.tensor_copy(srf[:, :, :], sr[:, :, :]).then_inc(rows_ready, 1)
            ch.wait()
            ch(nc.vector.tensor_reduce(lo[:, :], drf[:, :, :], AX, ALU.min))
            ch.link(nc.vector.tensor_reduce(hi[:, :], drf[:, :, :], AX, ALU.max))
            ch(nc.vector.tensor_copy(lo_i[:, :], lo[:, :]))
            ch(nc.vector.tensor_tensor(span[:, :], hi[:, :], lo[:, :], ALU.subtract))
            nc.vector.tensor_tensor(nodes[:, :, :], lo[:, :].unsqueeze(2).to_broadcast([STEPS, C4, WIN]),
                                    s.iota_w[0:STEPS, :].unsqueeze(1).to_broadcast([STEPS, C4, WIN]), ALU.add).then_inc(win_ready, 1)
            nc.vector.tensor_copy(lox[:, :, :], lo[:, :].unsqueeze(2).to_broadcast([STEPS, C4, R1])).then_inc(lox_ready, 1)
            ch.link(nc.vector.tensor_scalar(slot_i[:, :], slot_i[:, :], R1 - 1, 1, ALU.bitwise_and, ALU.logical_shift_right))
            ch(nc.vector.tensor_copy(slot[:, :], slot_i[:, :]))
            ve.wait_ge(vec_in, 48)
            ch(nc.vector.tensor_scalar(vv[:, 0:D], nv["v_in"], EPS, None, ALU.add))
            ch(nc.vector.tensor_scalar(vv[:, D:2 * D], nv["v_out"], EPS, None, ALU.add))
            ch(nc.vector.tensor_scalar(vv[:, 2 * D:], small[:, 3, :], EPS, None, ALU.add))
            nc.vector.tensor_scalar(upt[:, 1:2], up[:, 3:4], EPS, None, ALU.add).then_inc(sqrt_in, 1)
            ve.wait_ge(x_in, 16)
            ch.link(nc.vector.tensor_copy(s.xres[:, :, :], s.h[:, :, :]))
            normalised(nc, ve, ch, sqrt_in, sqrt_done, (s.mean, s.var, s.rs, s.tmp4, s.sq), s.xres, s.h, 3)
            rsqrt_refined(nc, ch, vr[:, :], vv[:, :], vt[:, :])
            rsqrt_refined(nc, ch, upt[:, 0:1], upt[:, 1:2], upt[:, 2:3])
            ch.link(nc.vector.tensor_tensor(vr[:, 0:D], vr[:, 0:D], nv["g_in"], ALU.mult))
            ch.link(nc.vector.tensor_tensor(cin[:, :], nv["m_in"], vr[:, 0:D], ALU.mult))
            ch.link(nc.vector.tensor_tensor(cin[:, :], nv["be_in"], cin[:, :], ALU.subtract))
            ch.link(nc.vector.tensor_tensor(s.h[:, :, :], s.h[:, :, :], vr[:, 0:D].unsqueeze(1).to_broadcast([NP, NB, D]), ALU.mult))
            ch.link(nc.vector.tensor_tensor(s.h[:, :, :], s.h[:, :, :], cin[:, :].unsqueeze(1).to_broadcast([NP, NB, D]), ALU.add))
            nc.vector.tensor_scalar(s.h[:, :, :], s.h[:, :, :], 0.0, None, ALU.max).then_inc(h_ready, 1)
            ch.link(nc.vector.tensor_tensor(vr[:, 2 * D:], vr[:, 2 * D:], small[:, 0, :], ALU.mult))
            ch.link(nc.vector.tensor_tensor(cmsg[:, :], small[:, 4, :], small[:, 2, :], ALU.subtract))
            ch.link(nc.vector.tensor_tensor(cmsg[:, :], cmsg[:, :], vr[:, 2 * D:], ALU.mult))
            ch.link(nc.vector.tensor_tensor(cmsg[:, :], cmsg[:, :], small[:, 1, :], ALU.add))
            ve.wait_ge(weights_in, 32)
            ch.link(nc.vector.tensor_tensor(vr[:, D:2 * D], vr[:, D:2 * D], nv["g_out"], ALU.mult))
            ch(nc.vector.tensor_tensor(s.w2s[:, :], s.w2s[:, :], vr[0:H0, D:2 * D], ALU.mult))
            ch.link(nc.vector.tensor_tensor(cin[:, :], nv["b2"], nv["m_out"], ALU.subtract))
            ch.link(nc.vector.tensor_tensor(cin[:, :], cin[:, :], vr[:, D:2 * D], ALU.mult))
            ch.link(nc.vector.tensor_tensor(cin[:, :], cin[:, :], nv["be_out"], ALU.add))
            ch(nc.vector.tensor_tensor(s.xres[:, :, :], s.xres[:, :, :], cin[:, :].unsqueeze(1).to_broadcast([NP, NB, D]), ALU.add))
            ch.link(nc.vector.tensor_tensor(s.upd_ab[:, 0:1], upt[:, 0:1], up[:, 0:1], ALU.mult))
            ch.link(nc.vector.tensor_tensor(upt[:, 3:4], up[:, 2:3], s.upd_ab[:, 0:1], ALU.mult))
            ch(nc.vector.tensor_tensor(s.upd_ab[:, 1:2], up[:, 1:2], upt[:, 3:4], ALU.subtract))
            ve.wait_ge(edge_in, 16 * 8)
            ch(nc.vector.tensor_copy(s.src_f[:, :], s.src_i[:, :]))
            ch.link(nc.vector.tensor_copy(s.dl[:, :], dst_i[:, :]))
            ve.wait_ge(wn_done, 1)
            ch(nc.vector.tensor_scalar(s.wn[:, :], s.ps[3][:, 0:STEPS], slot[:, :], None, ALU.add))
            ch(nc.vector.tensor_scalar(s.wn0[:, :], s.ps[3][:, 0:STEPS], slot[:, :], None, ALU.add))
            ve.wait_ge(win_in, 64)
            ch(nc.vector.tensor_copy(s.start[:, :], s.lo_i[:, :]))
            ch(nc.vector.tensor_tensor(s.dl[:, :], s.dl[:, :], lob[:, :], ALU.subtract))
            ch.link(nc.vector.tensor_reduce(span1[:, :], spans[:, :], AX, ALU.max))
            for win, rounds in ((WIN, s.rounds), (WIN1, s.rounds1)):
                ch.link(nc.vector.tensor_scalar(over[:, :], s.iota_n[0:1, 0:ROUNDS], float(win), float(win), ALU.mult, ALU.add))
                ch.link(nc.vector.tensor_scalar(over[:, :], over[:, :], span1[:, :], None, ALU.is_le))
                ch.link(nc.vector.tensor_reduce(count[:, :], over[:, :], AX, ALU.add))
                ch.link(nc.vector.tensor_copy(rounds[:, :], count[:, :]))
            ch(nc.vector.memset(s.updT[:, :], 0.0))
            ve.wait_ge(mm_done, 1)
            ch.link(nc.vector.tensor_tensor(Mf[:, :, :], s.ps[2][0:NP, 0:NB * H0].rearrange("p (b j) -> p b j", j=H0),
                                            vr[:, 2 * D:].unsqueeze(1).to_broadcast([NP, NB, H0]), ALU.mult))
            ch.link(nc.vector.tensor_tensor(Mf[:, :, :], Mf[:, :, :],
                                            cmsg[:, :].unsqueeze(1).to_broadcast([NP, NB, H0]), ALU.add))
            ch.link(nc.vector.tensor_scalar(Mf[:, :, :], Mf[:, :, :], 0.0, None, ALU.max))
            ch.link(nc.vector.tensor_copy(Mt[:, :, 0:H0], Mf[:, :, :]))
            nc.vector.tensor_tensor(Mt[:, :, H0:], Mf[:, :, :], Mt[:, :, 0:H0].bitcast(F), ALU.subtract).then_inc(m_ready, 1)

        @block.tensor
        def _(pe):
            pe.wait_ge(pool, 7)
            pe.wait_ge(lox_ready, 1)
            nc.tensor.transpose(s.ps[3][:, 0:STEPS], lox[:, :, :].rearrange("g a r -> g (a r)"), s.ident[0:STEPS, 0:STEPS]).then_inc(wn_done, 1)
            pe.wait_ge(h_ready, 1)
            for k in range(2):
                for b in range(NB):
                    last = nc.tensor.transpose(s.ps[k][:, b * NP:(b + 1) * NP], s.h[:, b, k * P:(k + 1) * P], s.ident[0:NP, 0:NP])
                last.then_inc(hT_done, 1)
            pe.wait_ge(weights_in, 32)
            pe.wait_ge(hT_ready, 2)
            for b in range(NB):
                for k in range(2):
                    last = nc.tensor.matmul(s.ps[2][0:NP, b * H0:(b + 1) * H0], s.hT[:, k, b, :], w1[:, k, :],
                                            start=(k == 0), stop=(k == 1))
            last.then_inc(mm_done, 1)


def stage_edges0(nc, a, s, mtab, eh_d):
    with ExitStack() as ctx:
        def sb(name, shape, dt=F):
            return ctx.enter_context(nc.sbuf_tensor(name, shape, dt))

        def sem(name):
            return ctx.enter_context(nc.semaphore(name))

        def each(f, name, *args):
            return [f(f"{name}{u}", *args) for u in range(BUF0)]

        ea = each(sb, "ea", [P, 2, GE])
        hi = each(sb, "ehi", [P, GE])
        eh = each(sb, "eh", [P, GE], FR)
        idx = each(sb, "idx", [P, A], I32)
        mg = each(sb, "mg", [P, A, 2 * H0], FR)
        hidT = each(sb, "hidT", [KH, GE])
        wh = each(sb, "wh", [P, A, KI])
        wp = each(sb, "wp", [P, 2, A, KI])
        mask = each(sb, "mask", [P, A, WIN])
        X = each(sb, "X", [P, A, 2, KI, WIN], FR)
        Ts = sb("Ts", [P, IPS, H0])
        BT = sb("BT", [P, KI, CS])
        CT = sb("CT", [KI, CS])
        UT = sb("UT", [H0, CS])
        U = sb("U", [PC, NPC, H0])
        sel = sb("sel", [PC, NPC, N])
        ea_in = each(sem, "ea_in")
        eh_out = each(sem, "eh_out")
        mg_in = [[sem(f"mg_in{u}{c}") for c in range(A)] for u in range(BUF0)]
        idx_ready = sem("idx_ready")
        hidT_done = sem("hidT_done")
        hidT_kept = sem("hidT_kept")
        hid_done = sem("hid_done")
        hi_ready = sem("hi_ready")
        eh_ready = sem("eh_ready")
        wh_ready = sem("wh_ready")
        wp_ready = sem("wp_ready")
        x_ready = sem("x_ready")
        bt_done = sem("bt_done")
        bt_kept = sem("bt_kept")
        ts_ready = sem("ts_ready")
        ts_used = sem("ts_used")
        ut_done = sem("ut_done")
        ut_kept = sem("ut_kept")
        u_done = sem("u_done")
        u_kept = sem("u_kept")
        sel_ready = sem("sel_ready")
        upd_done = sem("upd_done")
        round_done = sem("round_done")
        waited = sem("waited0")
        waited_act = sem("waited0_act")
        block = ctx.enter_context(nc.Block())
        FREE = BUF0
        YW = XW + WIN

        def rounds(eng):
            return eng.value_load(s.rounds[0:1, 0:1], min_val=0, max_val=ROUNDS - 1) + 1

        @block.sync
        def _(sp):
            def load(t, u):
                g = t * BUF0 + u
                sp.dma_start(ea[u][:, :, :].rearrange("p a e -> p (a e)"), a["ea"][:, ds(g * (2 * GE), 2 * GE)]).then_inc(ea_in[u], 16)

            def store(r, t, u):
                g = t * BUF0 + u
                sp.wait_ge(eh_ready, r * GR + g + (FREE + 1))
                sp.dma_start(eh_d[:, ds(g, 1), :].rearrange("p g e -> p (g e)"), eh[u][:, :].bitcast(F)).then_inc(eh_out[u], 16)

            with sp.Fori(0, rounds(sp)) as r:
                for u in range(BUF0):
                    sp.wait_ge(hidT_done, r * GR + u + 1)
                    sp.wait_ge(eh_ready, r * GR + u + 1)
                    load(0, u)
                with sp.Fori(0, STEPS0 - 1) as t:
                    for u in range(BUF0):
                        sp.wait_ge(hidT_done, r * GR + t * BUF0 + u + (FREE + 1))
                        sp.wait_ge(eh_ready, r * GR + t * BUF0 + u + (FREE + 1))
                        load(t + 1, u)
                        store(r, t, u)
                for u in range(BUF0):
                    store(r, STEPS0 - 1, u)
                for u in range(BUF0):
                    sp.wait_ge(eh_out[u], (r + 1) * (16 * STEPS0))
                sp.wait_ge(round_done, r + 1)

        @block.gpsimd
        def _(pl):
            with pl.Fori(0, rounds(pl)) as r:
                with pl.Fori(0, STEPS0) as t:
                    for u in range(BUF0):
                        g = t * BUF0 + u
                        pl.wait_ge(idx_ready, r * GR + g + 1)
                        for c in range(A):
                            pl.wait_ge(bt_done, (r * GR + g) * A + c + 1)
                            pl.sem_inc(waited, 1)
                            pl.indirect_dma_start(mg[u][:, c, :].bitcast(F), None, mtab, bass.IndirectOffsetOnAxis(idx[u][:, c:c + 1], 0))\
                              .then_inc(mg_in[u][c], 16)

        @block.tensor
        def _(pe):
            pe.sem_inc(hidT_done, FREE)
            pe.sem_inc(hid_done, FREE)
            pe.sem_inc(bt_done, FREE * A)
            pe.sem_inc(ts_used, 1)

            def hidden(r, t, u):
                g = t * BUF0 + u
                pe.wait_ge(ea_in[u], (r * STEPS0 + t) * 16 + 16)
                pe.wait_ge(hidT_kept, r * GR + g + 1)
                nc.tensor.matmul(s.ps[3 + u][0:KH, 0:GE], s.kw1[:, :], ea[u][:, 0, :], start=True, stop=True).then_inc(hidT_done, 1)

            def turned(r, t, u):
                g = t * BUF0 + u
                pe.wait_ge(hidT_kept, r * GR + g + (FREE + 1))
                pe.wait_ge(wh_ready, r * GR + g + 1)
                pe.sem_inc(waited, 1)
                for c in range(A):
                    last = nc.tensor.transpose(s.ps[3 + u][:, GE + c * KH:GE + (c + 1) * KH], hidT[u][:, c * P:(c + 1) * P], s.ident[0:KH, 0:KH])
                last.then_inc(hid_done, 1)

            def sums(r, t, u):
                g = t * BUF0 + u
                pe.wait_ge(bt_kept, r * GR + g + 1)
                for c in range(A):
                    pe.wait_ge(mg_in[u][c], (r * STEPS0 + t) * 16 + 16)
                    pe.wait_ge(x_ready, (r * GR + g) * A + c + 1)
                    for part in range(2):
                        nc.tensor.matmul(s.ps[u][:, c * YW:c * YW + XW], mg[u][:, c, :], X[u][:, c, part, :, :].rearrange("p i w -> p (i w)"),
                                         start=(part == 0), stop=(part == 1))
                    nc.tensor.matmul(s.ps[u][0:KI, c * YW + XW:(c + 1) * YW], wh[u][:, c, :], mask[u][:, c, :],
                                     start=True, stop=True).then_inc(bt_done, 1)

            def edges_T(r, n, i, seg, first, last_i):
                for j in range(IPS):
                    last = nc.tensor.matmul(s.ps[6][0:H0, 0:SC], Ts[:, j, :], BT[:, ds(i * IPS + j, 1), ds(seg * SC, SC)].rearrange("p i c -> p (i c)"),
                                            start=(first and j == 0), stop=False)
                last.then_inc(ts_used, 1)

            def step(r, t):
                for u in range(BUF0):
                    turned(r, t + (u + 1) // BUF0, (u + 1) % BUF0)
                    hidden(r, t + (u + 2) // BUF0, (u + 2) % BUF0)
                    sums(r, t, u)

            def apply_T(r, seg, i, start=False):
                pe.wait_ge(ts_ready, (r * SEGS + seg) * SEG + i + 1)
                edges_T(r, None, i, seg, start, None)

            def apply_T0(r, seg):
                nc.tensor.matmul(s.ps[6][0:H0, 0:SC], s.T0[:, :], CT[:, ds(seg * SC, SC)], start=False, stop=True).then_inc(ut_done, 1)

            with pe.Fori(0, rounds(pe)) as r:
                hidden(r, 0, 0)
                turned(r, 0, 0)
                hidden(r, 0, 1)
                with pe.Fori(0, SEG) as t:
                    step(r, t)
                pe.wait_ge(bt_kept, r * GR + SEG * BUF0 + FREE)
                pe.wait_ge(ut_kept, r * SEGS + 1)
                step(r, SEG)
                apply_T(r, 0, 0, True)
                with pe.Fori(1, SEG - 1) as i:
                    step(r, SEG + i)
                    apply_T(r, 0, i)
                turned(r, STEPS0 - 1, 1)
                hidden(r, STEPS0 - 1, 2)
                sums(r, STEPS0 - 1, 0)
                turned(r, STEPS0 - 1, 2)
                sums(r, STEPS0 - 1, 1)
                sums(r, STEPS0 - 1, 2)
                apply_T(r, 0, SEG - 1)
                apply_T0(r, 0)
                pe.wait_ge(bt_kept, r * GR + GR + FREE)
                pe.wait_ge(ut_kept, r * SEGS + 2)
                apply_T(r, 1, 0, True)
                with pe.Fori(1, SEG) as i:
                    apply_T(r, 1, i)
                apply_T0(r, 1)
                pe.wait_ge(ut_kept, r * SEGS + (SEGS + 1))
                pe.sem_inc(waited, 1)
                for j in range(NPC):
                    last = nc.tensor.transpose(s.ps[7][0:PC, j * H0:(j + 1) * H0], UT[:, j:CS:NPC], s.ident[0:H0, 0:H0])
                last.then_inc(u_done, 1)
                pe.wait_ge(u_kept, r + 1)
                pe.wait_ge(sel_ready, r + 1)
                for j in range(NPC):
                    last = nc.tensor.matmul(s.ps[6][0:H0, 0:N], U[:, j, :], sel[:, j, :], start=(j == 0), stop=(j == NPC - 1))
                last.then_inc(upd_done, 1)
                pe.wait_ge(round_done, r + 1)

        @block.scalar
        def _(act):
            act.sem_inc(hidT_kept, FREE)
            act.sem_inc(bt_kept, FREE)
            act.sem_inc(ut_kept, 1)

            def indices(r, t, u):
                for c in range(A):
                    act.wait_ge(mg_in[u][c], (r * STEPS0 + t) * 16)
                nc.scalar.copy(idx[u][:, :], s.src_i[:, ds((t * BUF0 + u) * A, A)]).then_inc(idx_ready, 1)

            def prepare(r, t, u):
                g = t * BUF0 + u
                act.wait_ge(hidT_done, r * GR + g + (FREE + 1))
                act.wait_ge(hid_done, r * GR + g + 1)
                nc.scalar.activation(hidT[u][:, :], s.ps[3 + u][0:KH, 0:GE], ACT.Relu, bias=s.kb1[:, :]).then_inc(hidT_kept, 1)
                act.wait_ge(eh_out[u], (r * STEPS0 + t) * 16)
                act.wait_ge(eh_ready, r * GR + g + 1)
                nc.scalar.activation(eh[u][0:DE1, :], ea[u][0:DE1, 1, :], ACT.Copy)
                nc.scalar.activation(hi[u][DE1:P, :].bitcast(FR), ea[u][DE1:P, 1, :], ACT.Copy).then_inc(hi_ready, 1)

            def keep(r, t, u):
                g = t * BUF0 + u
                act.wait_ge(bt_done, (r * GR + g) * A + (FREE * A + A))
                at = g * (A * WIN)
                for c in range(A):
                    nc.scalar.activation(BT[:, :, ds(at + c * WIN, WIN)], s.ps[u][:, c * YW:c * YW + XW].rearrange("p (i w) -> p i w", w=WIN), ACT.Copy)
                nc.scalar.activation(CT[:, ds(at, A * WIN)].rearrange("p (c w) -> p c w", c=A),
                                     s.ps[u][0:KI, 0:A * YW].rearrange("p (c y) -> p c y", c=A)[:, :, XW:YW], ACT.Copy).then_inc(bt_kept, 1)

            def load_T(r, v, i):
                act.wait_ge(ts_used, (r * SEGS + v) * SEG + i + 1)
                nc.scalar.copy(Ts[:, :, :], s.T[:, ds(i * IPS, IPS), :]).then_inc(ts_ready, 1)

            def keep_UT(r, v):
                act.wait_ge(ut_done, r * SEGS + v + 1)
                nc.scalar.activation(UT[:, ds(v * SC, SC)], s.ps[6][0:H0, 0:SC], ACT.Copy).then_inc(ut_kept, 1)

            def step(r, t):
                for u in range(BUF0):
                    indices(r, t + 1, u)
                    keep(r, t, u)
                    prepare(r, t + 1, u)

            with act.Fori(0, rounds(act)) as r:
                for u in range(BUF0):
                    indices(r, 0, u)
                for u in range(BUF0):
                    prepare(r, 0, u)
                with act.Fori(0, SEG) as t:
                    step(r, t)
                with act.Fori(0, SEG - 1) as i:
                    load_T(r, 0, i)
                    step(r, SEG + i)
                load_T(r, 0, SEG - 1)
                for u in range(BUF0):
                    keep(r, STEPS0 - 1, u)
                keep_UT(r, 0)
                with act.Fori(0, SEG) as i:
                    load_T(r, 1, i)
                keep_UT(r, 1)
                act.wait_ge(u_done, r + 1)
                nc.scalar.activation(U[:, :, :].rearrange("p a j -> p (a j)"), s.ps[7][0:PC, 0:NPC * H0], ACT.Copy).then_inc(u_kept, 1)
                act.wait_ge(round_done, r + 1)
                act.sem_inc(waited_act, 1)

        @block.vector
        def _(ve):
            ve.sem_inc(eh_ready, FREE)
            ve.sem_inc(wh_ready, FREE)
            with ve.Fori(0, rounds(ve)) as r:
                with ve.Fori(0, STEPS0) as t:
                    for u in range(BUF0):
                        g = t * BUF0 + u
                        n = r * GR + g
                        ve.wait_ge(bt_done, n * A + A)
                        nc.vector.tensor_tensor(mask[u][:, :, :], s.dl[:, ds(g * A, A)].unsqueeze(2).to_broadcast([P, A, WIN]),
                                                s.iota_w[:, :].unsqueeze(1).to_broadcast([P, A, WIN]), ALU.is_equal)
                        nc.vector.tensor_copy(wh[u][:, :, KH], s.w[:, ds(g * A, A)])
                        ve.wait_ge(hid_done, n + (FREE + 1))
                        nc.vector.tensor_tensor(wh[u][:, :, 0:KH], s.ps[3 + u][:, GE:GE + A * KH].rearrange("p (a i) -> p a i", a=A),
                                                s.w[:, ds(g * A, A)].unsqueeze(2).to_broadcast([P, A, KH]), ALU.mult).then_inc(wh_ready, 1)
                        ve.wait_ge(wh_ready, n + (FREE + 1))
                        nc.vector.tensor_copy(wp[u][:, 0, :, :].bitcast(FR), wh[u][:, :, :]).then_inc(wp_ready, 1)
                        ve.wait_ge(hi_ready, n + 1)
                        nc.vector.tensor_tensor(eh[u][DE1:P, :], ea[u][DE1:P, 1, :], hi[u][DE1:P, :], ALU.subtract).then_inc(eh_ready, 1)
                        ve.wait_ge(wp_ready, n * 2 + 1)
                        nc.vector.tensor_tensor(wp[u][:, 1, :, :].bitcast(FR), wh[u][:, :, :], wp[u][:, 0, :, :], ALU.subtract).then_inc(wp_ready, 1)
                        ve.wait_ge(wp_ready, n * 2 + 2)
                        for c in range(A):
                            nc.vector.tensor_tensor(X[u][:, c, :, :, :], wp[u][:, :, c, :].unsqueeze(3).to_broadcast([P, 2, KI, WIN]),
                                                    mask[u][:, c, :].unsqueeze(1).unsqueeze(1).to_broadcast([P, 2, KI, WIN]),
                                                    ALU.mult).then_inc(x_ready, 1)
                for j in range(NPC):
                    last = nc.vector.tensor_scalar(sel[:, j, :], s.iota_n[0:PC, :], s.node[:, j:j + 1], None, ALU.is_equal)
                last.then_inc(sel_ready, 1)
                ve.wait_ge(upd_done, r + 1)
                ve.wait_ge(sel_ready, r + 1)
                nc.vector.tensor_scalar(s.node[:, :], s.node[:, :], float(WIN), None, ALU.add)
                nc.vector.tensor_scalar(s.dl[:, :], s.dl[:, :], float(-WIN), None, ALU.add)
                nc.vector.tensor_tensor(s.updT[:, :], s.ps[6][0:H0, 0:N], s.updT[:, :], ALU.add).then_inc(round_done, 1)
                ve.wait_ge(round_done, r + 1)


def stage_nodes1(nc, a, s, qtab, ktab, vtab):
    with ExitStack() as ctx:
        def sb(name, shape, dt=F):
            return ctx.enter_context(nc.sbuf_tensor(name, shape, dt))

        def sem(name):
            return ctx.enter_context(nc.semaphore(name))

        s.mean = sb("mean1", [NP, NB])
        s.var = sb("var1", [NP, NB])
        s.rs = sb("rs1", [NP, NB])
        s.tmp4 = sb("tmp41", [NP, NB])
        s.h = sb("h1", [NP, NB, D])
        s.sq = sb("sq1", [NP, NB, D])
        s.hT = sb("hT1", [P, 2, NB, NP])
        vec = sb("vec1", [NP, len(VECS1), D])
        W = sb("Wqkv", [P, 2, 3, D])
        kb = sb("kb", [NP, D])
        kvf = sb("kvf", [NP, 2, NB, D])
        kv = sb("kv", [NP, 2, NB, 2, D])
        hi_ready = sem("kv_hi_ready")
        sum_ready = sem("kv_sum_ready")
        q_ready = sem("q_ready")
        qf = sb("qf", [NP, NB, D])
        updR = sb("updR", [H0, N])
        w_in = sem("w_in")
        vec_in = sem("vec1_in")
        upd_ready = sem("upd_ready")
        out0_done = sem("out0_done")
        h_ready = sem("h1_ready")
        hT_done = sem("h1T_done")
        hT_ready = sem("h1T_ready")
        qkv_done = sem("qkv_done")
        kv_ready = sem("kv_ready")
        kv_out = sem("kv_out")
        dve = sem("dve_done1")
        sqrt_in = sem("sqrt1_in")
        sqrt_done = sem("sqrt1_done")
        block = ctx.enter_context(nc.Block())

        @block.sync
        def _(sp):
            sp.dma_start(vec[:, :, :].rearrange("p a d -> p (a d)"), a["vecs1"].to_broadcast([NP, len(VECS1) * D])).then_inc(vec_in, 16)
            for i, n in enumerate(("Wq", "Wk", "Wv")):
                sp.dma_start(W[:, :, i, :], a[n].rearrange("(k p) j -> p k j", p=P)).then_inc(w_in, 16)
            sp.wait_ge(q_ready, 1)
            sp.dma_start(qtab.rearrange("(b p) d -> p b d", p=NP), qf[:, :, :]).then_inc(kv_out, 16)
            for i, tab in enumerate((ktab, vtab)):
                sp.wait_ge(kv_ready, i + 1)
                sp.dma_start(tab[0:N, :].rearrange("(b p) d -> p b d", p=NP), kv[:, i, :, :, :].rearrange("p b h d -> p b (h d)")).then_inc(kv_out, 16)
            sp.wait_ge(kv_out, 48)

        @block.scalar
        def _(act):
            act.activation(updR[:, :], s.updT[:, :], ACT.Relu, bias=s.upd_ab[:, 1:2], scale=s.upd_ab[:, 0:1]).then_inc(upd_ready, 1)
            act.wait_ge(sqrt_in, 1)
            act.activation(s.rs[:, :], s.var[:, :], ACT.Sqrt).then_inc(sqrt_done, 1)
            act.wait_ge(hT_done, 2)
            for k in range(2):
                act.activation(s.hT[:, k, :, :].rearrange("p b n -> p (b n)"), s.ps[2 + k][:, 0:N], ACT.Copy).then_inc(hT_ready, 1)
            for i in range(2):
                act.wait_ge(sum_ready, i + 1)
                act.activation(kv[:, i, :, 0, :].bitcast(FR), kvf[:, i, :, :], ACT.Copy).then_inc(hi_ready, 1)

        @block.tensor
        def _(pe):
            pe.wait_ge(upd_ready, 1)
            for b in range(NB):
                last = nc.tensor.matmul(s.ps[b // 2][0:NP, (b % 2) * D:(b % 2 + 1) * D], updR[:, b * NP:(b + 1) * NP], s.w2s[:, :],
                                        start=True, stop=True)
            last.then_inc(out0_done, 1)
            pe.wait_ge(h_ready, 1)
            for k in range(2):
                for b in range(NB):
                    last = nc.tensor.transpose(s.ps[2 + k][:, b * NP:(b + 1) * NP], s.h[:, b, k * P:(k + 1) * P], s.ident[0:NP, 0:NP])
                last.then_inc(hT_done, 1)
            pe.wait_ge(hT_ready, 2)
            pe.wait_ge(w_in, 48)
            for i in range(3):
                for b in range(NB):
                    bank = s.ps[(4, 6, 0)[i] + b // 2]
                    for k in range(2):
                        last = nc.tensor.matmul(bank[0:NP, (b % 2) * D:(b % 2 + 1) * D], s.hT[:, k, b, :], W[:, k, i, :],
                                                start=(k == 0), stop=(k == 1))
                last.then_inc(qkv_done, 1)

        @block.vector
        def _(ve):
            ch = Chain(ve, dve)
            nv = {n: vec[:, i, :] for i, n in enumerate(VECS1)}
            ve.wait_ge(vec_in, 16)
            ch.link(nc.vector.tensor_tensor(kb[:, :], nv["bk"], nv["be"], ALU.add))
            ve.wait_ge(out0_done, 1)
            for b in range(2):
                ch(nc.vector.tensor_tensor(s.xres[:, 2 * b:2 * b + 2, :], s.ps[b][0:NP, :].rearrange("p (b d) -> p b d", b=2),
                                           s.xres[:, 2 * b:2 * b + 2, :], ALU.add))
            ch.wait()
            normalised(nc, ve, ch, sqrt_in, sqrt_done, (s.mean, s.var, s.rs, s.tmp4, s.sq), s.xres, s.h, 1, h_ready)
            ch.link(nc.vector.tensor_tensor(s.xres[:, :, :], s.xres[:, :, :], nv["bias"].unsqueeze(1).to_broadcast([NP, NB, D]), ALU.add))
            for i, (bias, to, ready) in enumerate(((nv["bq"], qf[:, :, :], q_ready), (kb[:, :], kvf[:, 0, :, :], sum_ready),
                                                   (nv["bv"], kvf[:, 1, :, :], sum_ready))):
                ve.wait_ge(qkv_done, i + 1)
                last = nc.vector.tensor_tensor(to.rearrange("p (a b) d -> p a b d", a=2), s.psum[0:NP, (4, 6, 0)[i]:(6, 8, 2)[i], :].rearrange("p a (b d) -> p a b d", b=2),
                                               bias.unsqueeze(1).unsqueeze(1).to_broadcast([NP, 2, 2, D]), ALU.add).then_inc(ready, 1)
                if i == 0:
                    ve.wait_ge(q_ready, 1)
                    ch.link(nc.vector.tensor_copy(s.QT[:, :, 0, :], qf[:, :, :]))
                    ch(nc.vector.tensor_tensor(s.QT[:, :, 1, :], qf[:, :, :], s.QT[:, :, 0, :].bitcast(F), ALU.subtract))
            for i in range(2):
                ve.wait_ge(hi_ready, i + 1)
                nc.vector.tensor_tensor(kv[:, i, :, 1, :].bitcast(FR), kvf[:, i, :, :], kv[:, i, :, 0, :], ALU.subtract).then_inc(kv_ready, 1)


def stage_scores(nc, a, s, qtab, ktab, eh_d, src_d, dst_d):
    with ExitStack() as ctx:
        def sb(name, shape, dt=F):
            return ctx.enter_context(nc.sbuf_tensor(name, shape, dt))

        def sem(name):
            return ctx.enter_context(nc.semaphore(name))

        def each(f, name, n, *args):
            return [f(f"{name}{u}", *args) for u in range(n)]

        We = sb("We", [P, D])
        Wp = sb("Wp", [P, 2, D], FR)
        eh = each(sb, "eh1", PAIRS, [P, 2, GE], FR)
        kw = each(sb, "kwin", PAIRS, [P, D], FR)
        mt = each(sb, "mt", PAIRS, [P, P], FR)
        srcb = sb("srcb", [NP, STEPS, P])
        ohT = each(sb, "ohT", PAIRS, [NP, NB, P], FR)
        idx = each(sb, "idx1", BUF1, [P, A], I32)
        qg = each(sb, "qg", BUF1, [P, A, D])
        pr = each(sb, "pr", 2, [P, A, D])
        part_sum = sb("part_sum", [P, CH, HEADS])
        we_in = sem("we_in")
        rows_in = sem("rows_in")
        eh_in = each(sem, "eh1_in", PAIRS)
        kw_in = [[sem(f"kw_in{u}{c}") for c in range(A)] for u in range(BUF1)]
        qg_in = [[sem(f"qg_in{u}{c}") for c in range(A)] for u in range(BUF1)]
        idx_ready = sem("idx1_ready")
        mt_ready = sem("mt_ready")
        oh_ready = sem("oh_ready")
        q_done = sem("q_done")
        q_kept = sem("q_kept")
        key_done = sem("key_done")
        pr_ready = sem("pr_ready")
        alpha_done = sem("alpha_done")
        wp_ready = sem("wp_ready")
        wh_ready = sem("we_hi_ready")
        round_done = sem("round1_done")
        waited = sem("waited1")
        waited_act = sem("waited1_act")
        block = ctx.enter_context(nc.Block())
        FREE = BUF1
        PE_Q = A - 1

        def past(n, depth):
            return n + (FREE + 1 - depth)

        def rounds(eng):
            return eng.value_load(s.rounds1[0:1, 0:1], min_val=0, max_val=N // WIN1) + 1

        def window(eng, t, u, c, ready=None):
            first = eng.value_load(s.start[0:1, ds((t * BUF1 + u) * A + c, 1)], min_val=0, max_val=N)
            if ready is not None:
                eng.wait_ge(key_done, ready)
            row = (u % 2 * A + c) * R1
            eng.dma_start(kw[u // 2][row:row + R1, :].bitcast(F), ktab.rearrange("n (h d) -> (n h) d", h=2)[ds(first * 2, R1), :])\
               .then_inc(kw_in[u][c], 16)

        @block.sync
        def _(sp):
            sp.dma_start(We[0:DE1, :], a["We"]).then_inc(we_in, 16)
            sp.dma_start(We[DE1:P, :], a["We"]).then_inc(we_in, 16)
            chunks = dst_d.rearrange("(t c e) -> c t e", c=2 * A, e=P)
            for c in range(2 * A):
                sp.dma_start(s.dstb[c * R1:(c + 1) * R1, :, :], chunks[c:c + 1, :, :].to_broadcast([R1, STEPS, P])).then_inc(rows_in, 16)
            sp.dma_start(srcb[:, :, :], src_d.rearrange("(t c e) -> c t e", c=2 * A, e=P)[2 * A - 1:2 * A, :, :].to_broadcast([NP, STEPS, P])).then_inc(rows_in, 16)
            with sp.Fori(0, rounds(sp)) as r:
                with sp.Fori(0, STEPS1) as t:
                    for v in range(PAIRS):
                        g = t * BUF1 + 2 * v
                        sp.wait_ge(key_done, past(r * GR + g + 1, BUF1))
                        sp.dma_start(eh[v][:, :, :].bitcast(F), eh_d[:, ds(g, 2), :]).then_inc(eh_in[v], 16)
                        for u in (2 * v, 2 * v + 1):
                            window(sp, t, u, 0)
                sp.wait_ge(round_done, r + 1)

        @block.gpsimd
        def _(pl):
            with pl.Fori(0, rounds(pl)) as r:
                with pl.Fori(0, STEPS1) as t:
                    for u in range(BUF1):
                        g = t * BUF1 + u
                        pl.wait_ge(pr_ready, past(r * GR + g, BUF1))
                        pl.wait_ge(idx_ready, r * GR + g + 1)
                        pl.sem_inc(waited, 1)
                        for c in range(A):
                            if (u % 2, c) != (1, PE_Q):
                                pl.indirect_dma_start(qg[u][:, c, :], None, qtab, bass.IndirectOffsetOnAxis(idx[u][:, c:c + 1], 0))\
                                  .then_inc(qg_in[u][c], 16)

        @block.scalar
        def _(act):
            AHEAD = BUF1 - 2

            def fetch(r, t, u):
                for c in range(1, A):
                    window(act, t, u, c, past(r * GR + t * BUF1 + u, BUF1))
                act.wait_ge(pr_ready, past(r * GR + t * BUF1 + u, BUF1))
                nc.scalar.copy(idx[u][:, :], s.src_i[:, ds((t * BUF1 + u) * A, A)]).then_inc(idx_ready, 1)

            def keep_queries(r, t, u):
                g = t * BUF1 + u
                act.wait_ge(q_done, (r * STEPS + t * PAIRS) + (u // 2 + PAIRS + 1))
                act.wait_ge(pr_ready, past(r * GR + g, BUF1))
                nc.scalar.activation(qg[u][:, PE_Q, :], s.ps[6 + u // 2 % 2][:, 0:D], ACT.Copy).then_inc(q_kept, 1)

            def step(r, t, last=False):
                for u in range(BUF1):
                    if not last or u + AHEAD < BUF1:
                        fetch(r, t + (u + AHEAD) // BUF1, (u + AHEAD) % BUF1)
                    if u % 2:
                        keep_queries(r, t, u)

            act.sem_inc(q_kept, 2)
            with act.Fori(0, rounds(act)) as r:
                for u in range(AHEAD):
                    fetch(r, 0, u)
                with act.Fori(0, STEPS1 - 1) as t:
                    step(r, t)
                step(r, STEPS1 - 1, True)
                act.wait_ge(round_done, r + 1)
                act.sem_inc(waited_act, 1)

        @block.tensor
        def _(pe):
            pe.sem_inc(key_done, FREE)
            pe.sem_inc(q_done, PAIRS)
            pe.wait_ge(wp_ready, 1)

            def queries(r, t, v):
                n = r * STEPS + t * PAIRS + v
                pe.wait_ge(oh_ready, n + 1)
                pe.wait_ge(q_kept, n + (2 if v == 0 else 1))
                for b in range(NB):
                    for part in range(2):
                        last = nc.tensor.matmul(s.ps[6 + v % 2][:, 0:D], ohT[v][:, b, :], s.QT[:, b, part, :],
                                                start=(b == 0 and part == 0), stop=(b == NB - 1 and part == 1))
                last.then_inc(q_done, 1)

            def keys(r, t, u):
                n = r * GR + t * BUF1 + u
                pe.wait_ge(eh_in[u // 2], (r * STEPS1 + t) * 16 + 16)
                pe.wait_ge(mt_ready, n + 1)
                pe.wait_ge(pr_ready, past(n, BANKS))
                for c in range(A):
                    for part in range(2):
                        nc.tensor.matmul(s.ps[u % BANKS * A + c][:, 0:D], eh[u // 2][:, u % 2, c * P:(c + 1) * P], Wp[:, part, :], start=(part == 0), stop=False)
                for c in range(A):
                    row = (u % 2 * A + c) * R1
                    pe.wait_ge(kw_in[u][c], (r * STEPS1 + t) * 16 + 16)
                    last = nc.tensor.matmul(s.ps[u % BANKS * A + c][:, 0:D], mt[u // 2][row:row + R1, :], kw[u // 2][row:row + R1, :], start=False, stop=True)
                last.then_inc(key_done, 1)

            with pe.Fori(0, rounds(pe)) as r:
                with pe.Fori(0, STEPS1) as t:
                    for v in range(PAIRS):
                        queries(r, t, v)
                        keys(r, t, 2 * v)
                        keys(r, t, 2 * v + 1)

        @block.vector
        def _(ve):
            ve.sem_inc(pr_ready, FREE)
            ve.sem_inc(alpha_done, 2)
            ve.wait_ge(we_in, 32)
            nc.vector.tensor_copy(Wp[:, 0, :], We[:, :]).then_inc(wh_ready, 1)
            nc.vector.memset(s.alpha[:, :, :], 0.0)
            ve.wait_ge(wh_ready, 1)
            nc.vector.tensor_tensor(Wp[:, 1, :], We[:, :], Wp[:, 0, :].bitcast(F), ALU.subtract).then_inc(wp_ready, 1)
            ve.wait_ge(rows_in, 16 * (2 * A + 1))

            def masks(r, t, u):
                n = r * GR + t * BUF1 + u
                rows = slice(u % 2 * A * R1, (u % 2 + 1) * A * R1)
                ve.wait_ge(key_done, past(n, BUF1))
                nc.vector.tensor_scalar(mt[u // 2][rows, :], s.dstb[rows, ds(t * PAIRS + u // 2, 1), :].rearrange("p t e -> p (t e)"),
                                        s.wn[rows, ds(t * PAIRS + u // 2, 1)], None, ALU.is_equal).then_inc(mt_ready, 1)

            def one_hot(r, t, v):
                ve.wait_ge(q_done, r * STEPS + t * PAIRS + v + 1)
                for b in range(NB):
                    last = nc.vector.tensor_scalar(ohT[v][:, b, :], srcb[:, ds(t * PAIRS + v, 1), :].rearrange("p t e -> p (t e)"),
                                                   s.nodeid[:, b:b + 1], None, ALU.is_equal)
                last.then_inc(oh_ready, 1)

            def scores(r, t, u):
                g = t * BUF1 + u
                for c in range(A):
                    if (u % 2, c) != (1, PE_Q):
                        ve.wait_ge(qg_in[u][c], (r * STEPS1 + t) * 16 + 16)
                    else:
                        ve.wait_ge(q_kept, (r * STEPS + t * PAIRS) + (u // 2 + 3))
                ve.wait_ge(key_done, past(r * GR + g, 0))
                ve.wait_ge(alpha_done, r * GR + g + 1)
                nc.vector.tensor_tensor(pr[u % 2][:, :, :], s.psum[:, u % BANKS * A:(u % BANKS + 1) * A, 0:D], qg[u][:, :, :], ALU.mult).then_inc(pr_ready, 1)

            def add(r, t, u):
                g = t * BUF1 + u
                ve.wait_ge(pr_ready, past(r * GR + g, 0))
                nc.vector.tensor_reduce(part_sum[:, ds(g * A, A), :].rearrange("p a h -> p (a h)"),
                                        pr[u % 2][:, :, :].rearrange("p a (h c) -> p (a h) c", c=C), AX, ALU.add).then_inc(alpha_done, 1)

            def ahead(r, t, v):
                masks(r, t, 2 * v)
                masks(r, t, 2 * v + 1)
                one_hot(r, t, v)

            def pair(r, t, v, more=True):
                scores(r, t, 2 * v)
                if more:
                    ahead(r, t + (v + 1) // PAIRS, (v + 1) % PAIRS)
                add(r, t, 2 * v)
                scores(r, t, 2 * v + 1)
                add(r, t, 2 * v + 1)

            with ve.Fori(0, rounds(ve)) as r:
                ahead(r, 0, 0)
                with ve.Fori(0, STEPS1 - 1) as t:
                    for v in range(PAIRS):
                        pair(r, t, v)
                for v in range(PAIRS):
                    pair(r, STEPS1 - 1, v, v < PAIRS - 1)
                ve.wait_ge(alpha_done, r * GR + GR + 2)
                nc.vector.memset(Wp[:, :, :].bitcast(F), 0.0)
                nc.vector.tensor_scalar(s.wn[:, :], s.wn[:, :], float(WIN1), None, ALU.add)
                nc.vector.tensor_scalar(s.start[:, :], s.start[:, :], float(WIN1), float(N), ALU.add, ALU.min)
                nc.vector.tensor_tensor(s.alpha[:, :, :], s.alpha[:, :, :], part_sum[:, :, :], ALU.add).then_inc(round_done, 1)
                ve.wait_ge(round_done, r + 1)


def stage_softmax(nc, a, s):
    with ExitStack() as ctx:
        def sb(name, shape, dt=F):
            return ctx.enter_context(nc.sbuf_tensor(name, shape, dt))

        def sem(name):
            return ctx.enter_context(nc.semaphore(name))

        pm = sb("pm", [P, HEADS])
        am = sb("am", [P, HEADS])
        sm = sb("sm", [P, HEADS])
        masked = sem("masked")
        pm_ready = sem("pm_ready")
        am_ready = sem("am_ready")
        shifted = sem("shifted")
        exp_done = sem("exp_done")
        sm_ready = sem("sm_ready")
        total_ready = sem("total_ready")
        rsum_ready = sem("rsum_ready")
        block = ctx.enter_context(nc.Block())
        by_head = s.alpha[:, :, :].rearrange("p c h -> p h c")
        first = E // P

        @block.gpsimd
        def _(pl):
            part = s.alpha[:, first:, :]
            nc.gpsimd.affine_select(out=part, in_=part, compare_op=ALU.is_ge, fill=-3.0e38, base=E - 1 - first * P,
                                    pattern=[[-P, CH - first], [0, HEADS]], channel_multiplier=-1).then_inc(masked, 1)
            pl.wait_ge(pm_ready, 1)
            nc.gpsimd.partition_all_reduce(am[:, :], pm[:, :], P, bass.bass_isa.ReduceOp.max).then_inc(am_ready, 1)
            pl.wait_ge(sm_ready, 1)
            nc.gpsimd.partition_all_reduce(pm[:, :], sm[:, :], P, bass.bass_isa.ReduceOp.add).then_inc(total_ready, 1)

        @block.vector
        def _(ve):
            nc.vector.tensor_copy(s.wn[:, :], s.wn0[:, :])
            nc.vector.tensor_copy(s.start[:, :], s.lo_i[:, :])
            ve.wait_ge(masked, 1)
            nc.vector.tensor_reduce(pm[:, :], by_head, AX, ALU.max).then_inc(pm_ready, 1)
            ve.wait_ge(am_ready, 1)
            nc.vector.tensor_tensor(s.alpha[:, :, :], s.alpha[:, :, :], am[:, :].unsqueeze(1).to_broadcast([P, CH, HEADS]),
                                    ALU.subtract).then_inc(shifted, 1)
            ve.wait_ge(exp_done, 1)
            nc.vector.tensor_reduce(sm[:, :], by_head, AX, ALU.add).then_inc(sm_ready, 1)
            ve.wait_ge(total_ready, 1)
            nc.vector.reciprocal(s.rsum[:, :], pm[:, :]).then_inc(rsum_ready, 1)

        @block.scalar
        def _(act):
            act.wait_ge(shifted, 1)
            act.activation(s.alpha[:, :, :], s.alpha[:, :, :], ACT.Exp, scale=float(C) ** -0.5).then_inc(exp_done, 1)


def stage_values(nc, a, s, vtab, out):
    with ExitStack() as ctx:
        def sb(name, shape, dt=F):
            return ctx.enter_context(nc.sbuf_tensor(name, shape, dt))

        def sem(name):
            return ctx.enter_context(nc.semaphore(name))

        def each(f, name, n, *args):
            return [f(f"{name}{u}", *args) for u in range(n)]

        vw = each(sb, "vwin", PAIRS, [P, D], FR)
        mt = each(sb, "mtv", PAIRS, [P, P], FR)
        pv = each(sb, "pv_", BANKS, [P, A, D])
        ph = each(sb, "ph_", BANKS, [P, A, D], FR)
        pl_ = each(sb, "pl_", BANKS, [P, A, D], FR)
        oh = each(sb, "oh_", BANKS, [P, A, N], FR)
        zero = sb("zero", [P, N])
        outT = sb("outT", [P, 2, N])
        scaled = sb("scaled", [NP, NB, D])
        res = sb("res", [NP, NB, D])
        vw_in = [[sem(f"vw_in{u}{c}") for c in range(A)] for u in range(BUF1)]
        mt_ready = sem("mt2_ready")
        vg_done = sem("vg_done")
        pv_ready = sem("pv_ready")
        ph_ready = sem("ph_ready")
        pl_ready = sem("pl_ready")
        oh_ready = sem("oh2_ready")
        sum_done = sem("sum_done")
        all_done = sem("all_done")
        outT_kept = sem("outT_kept")
        turned = sem("turned")
        zero_ready = sem("zero_ready")
        scaled_ready = sem("scaled_ready")
        res_ready = sem("res_ready")
        res_out = sem("res_out")
        round_done = sem("round2_done")
        waited = sem("waited2")
        block = ctx.enter_context(nc.Block())
        FREE = BUF1
        HALF = D // 2

        def past(n, depth):
            return n + (FREE + 1 - depth)

        def rounds(eng):
            return eng.value_load(s.rounds1[0:1, 0:1], min_val=0, max_val=N // WIN1) + 1

        def window(eng, r, t, u, c):
            g = t * BUF1 + u
            first = eng.value_load(s.start[0:1, ds(g * A + c, 1)], min_val=0, max_val=N)
            eng.wait_ge(vg_done, past(r * GR + g, BUF1))
            row = (u % 2 * A + c) * R1
            eng.dma_start(vw[u // 2][row:row + R1, :].bitcast(F), vtab.rearrange("n (h d) -> (n h) d", h=2)[ds(first * 2, R1), :])\
               .then_inc(vw_in[u][c], 16)

        @block.sync
        def _(sp):
            with sp.Fori(0, rounds(sp)) as r:
                with sp.Fori(0, STEPS1) as t:
                    for u in range(BUF1):
                        window(sp, r, t, u, 0)
                sp.wait_ge(round_done, r + 1)
            sp.wait_ge(res_ready, 1)
            sp.dma_start(out.rearrange("(b p) d -> p b d", p=NP), res[:, :, :]).then_inc(res_out, 16)
            sp.wait_ge(res_out, 16)

        @block.gpsimd
        def _(pl):
            pl.sem_inc(pl_ready, FREE)
            with pl.Fori(0, rounds(pl)) as r:
                with pl.Fori(0, STEPS1) as t:
                    for u in range(BUF1):
                        n = r * GR + t * BUF1 + u
                        b = u % BANKS
                        pl.wait_ge(ph_ready, past(n, 0))
                        pl.wait_ge(sum_done, past(n, BANKS))
                        nc.gpsimd.tensor_tensor(pl_[b][:, :, :], pv[b][:, :, :], ph[b][:, :, :].bitcast(F), ALU.subtract).then_inc(pl_ready, 1)

        @block.scalar
        def _(act):
            act.sem_inc(ph_ready, FREE)
            AHEAD = BUF1 - 2

            def step(r, t, last=False):
                for u in range(BUF1):
                    if not last or u + AHEAD < BUF1:
                        for c in range(1, A):
                            window(act, r, t + (u + AHEAD) // BUF1, (u + AHEAD) % BUF1, c)
                    n = r * GR + t * BUF1 + u
                    b = u % BANKS
                    act.wait_ge(pv_ready, past(n, 0))
                    act.wait_ge(sum_done, past(n, BANKS))
                    act.wait_ge(pl_ready, past(n, BANKS))
                    nc.scalar.activation(ph[b][:, :, :], pv[b][:, :, :], ACT.Copy).then_inc(ph_ready, 1)

            with act.Fori(0, rounds(act)) as r:
                for u in range(AHEAD):
                    for c in range(1, A):
                        window(act, r, 0, u, c)
                with act.Fori(0, STEPS1 - 1) as t:
                    step(r, t)
                step(r, STEPS1 - 1, True)
                act.wait_ge(round_done, r + 1)
                act.sem_inc(waited, 1)
            act.wait_ge(all_done, 1)
            for h in range(2):
                act.activation(outT[:, h, :], s.ps[6 + h][:, 0:N], ACT.Copy).then_inc(outT_kept, 1)

        @block.tensor
        def _(pe):
            pe.sem_inc(vg_done, FREE)
            pe.sem_inc(sum_done, FREE)
            pe.wait_ge(zero_ready, 1)
            for h in range(2):
                nc.tensor.matmul(s.ps[6 + h][:, 0:N], zero[:, 0:P], zero[:, :], start=True, stop=False)

            def values(r, t, u):
                n = r * GR + t * BUF1 + u
                pe.wait_ge(mt_ready, n + 1)
                pe.wait_ge(pv_ready, past(n, BANKS))
                for c in range(A):
                    row = (u % 2 * A + c) * R1
                    pe.wait_ge(vw_in[u][c], (r * STEPS1 + t) * 16 + 16)
                    last = nc.tensor.matmul(s.ps[u % BANKS * A + c][:, 0:D], mt[u // 2][row:row + R1, :], vw[u // 2][row:row + R1, :], start=True, stop=True)
                last.then_inc(vg_done, 1)

            def add(r, t, u):
                n = r * GR + t * BUF1 + u
                pe.wait_ge(oh_ready, n + 1)
                for part, ready in ((ph, ph_ready), (pl_, pl_ready)):
                    pe.wait_ge(ready, past(n, 0))
                    for c in range(A):
                        for h in range(2):
                            last = nc.tensor.matmul(s.ps[6 + h][:, 0:N], part[u % BANKS][:, c, h * HALF:(h + 1) * HALF], oh[u % BANKS][:, c, :],
                                                    start=False, stop=False)
                last.then_inc(sum_done, 1)

            def step(r, t, last=False):
                for u in range(BUF1):
                    if not last or u + 2 < BUF1:
                        values(r, t + (u + 2) // BUF1, (u + 2) % BUF1)
                    add(r, t, u)

            with pe.Fori(0, rounds(pe)) as r:
                values(r, 0, 0)
                values(r, 0, 1)
                with pe.Fori(0, STEPS1 - 1) as t:
                    step(r, t)
                step(r, STEPS1 - 1, True)
            for h in range(2):
                last = nc.tensor.matmul(s.ps[6 + h][:, 0:N], zero[:, 0:P], zero[:, :], start=False, stop=True)
            last.then_inc(all_done, 1)
            pe.wait_ge(outT_kept, 2)
            for b in range(NB):
                for h in range(2):
                    last = nc.tensor.transpose(s.ps[b][0:NP, h * HALF:(h + 1) * HALF], outT[:, h, b * NP:(b + 1) * NP], s.ident[:, :])
            last.then_inc(turned, 1)

        @block.vector
        def _(ve):
            ve.sem_inc(pv_ready, FREE)
            nc.vector.memset(zero[:, :], 0.0).then_inc(zero_ready, 1)

            def masks(r, t, u):
                rows = slice(u % 2 * A * R1, (u % 2 + 1) * A * R1)
                ve.wait_ge(vg_done, past(r * GR + t * BUF1 + u, BUF1))
                nc.vector.tensor_scalar(mt[u // 2][rows, :], s.dstb[rows, ds(t * PAIRS + u // 2, 1), :].rearrange("p t e -> p (t e)"),
                                        s.wn[rows, ds(t * PAIRS + u // 2, 1)], None, ALU.is_equal).then_inc(mt_ready, 1)

            def weigh(r, t, u):
                g = t * BUF1 + u
                b = u % BANKS
                ve.wait_ge(vg_done, past(r * GR + g, 0))
                ve.wait_ge(pl_ready, past(r * GR + g, BANKS))
                nc.vector.tensor_tensor(pv[b][:, :, :].rearrange("p a (h c) -> p a h c", c=C),
                                        s.psum[:, b * A:(b + 1) * A, 0:D].rearrange("p a (h c) -> p a h c", c=C),
                                        s.alpha[:, ds(g * A, A), :].unsqueeze(3).to_broadcast([P, A, HEADS, C]),
                                        ALU.mult).then_inc(pv_ready, 1)

            def one_hot(r, t, u):
                g = t * BUF1 + u
                ve.wait_ge(sum_done, past(r * GR + g, BANKS))
                for c in range(A):
                    last = nc.vector.tensor_scalar(oh[u % BANKS][:, c, :], s.iota_n[:, :], s.src_f[:, ds(g * A + c, 1)], None, ALU.is_equal)
                last.then_inc(oh_ready, 1)

            def step(r, t, last=False):
                for u in range(BUF1):
                    weigh(r, t, u)
                    if not last or u + 3 < BUF1:
                        masks(r, t + (u + 3) // BUF1, (u + 3) % BUF1)
                    one_hot(r, t, u)

            with ve.Fori(0, rounds(ve)) as r:
                for u in range(3):
                    masks(r, 0, u)
                with ve.Fori(0, STEPS1 - 1) as t:
                    step(r, t)
                step(r, STEPS1 - 1, True)
                nc.vector.tensor_scalar(s.wn[:, :], s.wn[:, :], float(WIN1), None, ALU.add)
                nc.vector.tensor_scalar(s.start[:, :], s.start[:, :], float(WIN1), float(N), ALU.add, ALU.min).then_inc(round_done, 1)
                ve.wait_ge(round_done, r + 1)
            ve.wait_ge(turned, 1)
            nc.vector.tensor_tensor(scaled[:, :, :].rearrange("p b (h c) -> p b h c", c=C),
                                    s.psum[0:NP, 0:NB, 0:D].rearrange("p b (h c) -> p b h c", c=C),
                                    s.rsum[0:NP, :].unsqueeze(1).unsqueeze(3).to_broadcast([NP, NB, HEADS, C]), ALU.mult).then_inc(scaled_ready, 1)
            ve.wait_ge(scaled_ready, 1)
            nc.vector.tensor_tensor(res[:, :, :], scaled[:, :, :], s.xres[:, :, :], ALU.add).then_inc(res_ready, 1)


def kernel(**inputs):
    import numpy as np
    import concourse.bacc as bacc
    from concourse.bass_utils import run_bass_kernel_spmd

    x = {k: np.ascontiguousarray(v) for k, v in inputs.items()}
    l0 = {k[7:]: v for k, v in x.items() if k.startswith("L0_gnn_")}
    l1 = {k[7:]: v for k, v in x.items() if k.startswith("L1_gnn_")}

    def padded(v, fill):
        return np.pad(v, [(0, 0)] * (v.ndim - 1) + [(0, EP - E)], constant_values=fill)

    def per_chunk(v):
        return np.ascontiguousarray(v.reshape(CH, P).T)

    src, dst = padded(x["src"], 0), padded(x["dst"], N - 1)
    kw2 = l0["kw2"].reshape(KH, H0 + 1, H0)
    kb2 = l0["kb2"].reshape(1, H0 + 1, H0)
    rows = np.concatenate([kw2, kb2])
    ea128 = padded(x["edge_attr_128"].T, 0).reshape(P, GR, GE)
    ea64 = padded(x["edge_attr_64"].T, 0).reshape(DE1, GR, GE)
    arrays = {
        "x": x["x"],
        "src_pc": per_chunk(src),
        "dst_pc": per_chunk(dst),
        "src_rows": src.reshape(STEPS, 2 * A, P),
        "dst_rows": dst.reshape(STEPS, 2 * A, P),
        "w_pc": per_chunk(padded(x["edge_weight"], 0)),
        "ea": np.ascontiguousarray(np.stack([ea128, np.concatenate([ea64, ea64])], axis=2)).reshape(P, 2 * EP),
        "vecs0": np.concatenate([l0[n] for n in VECS0]).reshape(1, -1),
        "vecs1": np.concatenate([l1[n] for n in VECS1]).reshape(1, -1),
        "msg_vecs": np.concatenate([l0[n] for n in ("g_msg", "be_msg", "m_msg", "v_msg", "b1")]).reshape(1, -1),
        "upd_vecs": np.ascontiguousarray(np.stack([l0[n] for n in ("g_upd", "be_upd", "m_upd", "v_upd")], axis=1)),
        "w1": l0["w1"], "w2": l0["w2"], "kw1": l0["kw1"], "kb1": l0["kb1"].reshape(KH, 1),
        "T": np.ascontiguousarray(rows[:, 1:, :].transpose(2, 0, 1)),
        "T0": np.ascontiguousarray(rows[:, 0, :]),
        "Wq": l1["Wq"], "Wk": l1["Wk"], "Wv": l1["Wv"], "We": l1["We"],
    }
    nc = bacc.Bacc("TRN2", target_bir_lowering=False, num_devices=1)
    aps = {n: nc.dram_tensor(f"in_{n}", v.shape, mybir.dt.from_np(v.dtype), kind="ExternalInput").ap() for n, v in arrays.items()}
    out = nc.dram_tensor("out", [N, D], F, kind="ExternalOutput").ap()
    build(nc, aps, out)
    r = run_bass_kernel_spmd(nc, [{f"in_{n}": v for n, v in arrays.items()}], core_ids=[0])
    return r.results[0]["out"]
```
